# Optimizing a Trainium2 kernel written in Bass

```python
import numpy as np
import jax
import jax.numpy as jnp

def _softmax(x, axis=-1):
    return jax.nn.softmax(x, axis=axis)

def _gelu(x):
    return jax.nn.gelu(x, approximate=True)

def _silu(x):
    return jax.nn.silu(x)

def _sigmoid(x):
    return jax.nn.sigmoid(x)

def _layernorm(x, axis=-1, eps=1e-05):
    m = jnp.mean(x, axis=axis, keepdims=True)
    v = jnp.var(x, axis=axis, keepdims=True)
    return (x - m) / jnp.sqrt(v + eps)

def _scatter_add(tgt, idx, src, axis=0):
    return tgt.at[idx].add(src)

def _segment_sum(src, seg, n):
    return jax.ops.segment_sum(src, seg, n)
kernel_name = 'mk_prb_d2_jaxref_r8_8da1bd'

def setup_inputs(seed: int=0):
    np.random.seed(seed)
    _w = jnp.asarray

    def _L0_attn_setup():
        import jax, jax.numpy as jnp
        import numpy as np
        D_MODEL = 128
        D_STATE = 64
        HEADDIM = 64
        EXPAND = 2
        D_INNER = D_MODEL * EXPAND
        NHEADS = D_INNER // HEADDIM
        D_IN_PROJ = 2 * D_INNER + 2 * D_STATE + NHEADS
        BATCH, SEQLEN = (4, 512)

        def layernorm(x, w, b, eps=1e-05):
            mu = jnp.mean(x, axis=-1, keepdims=True)
            var = jnp.mean(jnp.square(x - mu), axis=-1, keepdims=True)
            return (x - mu) * jax.lax.rsqrt(var + eps) * w + b

        def _selective_scan(x_multi, A, Bm, Cm, dt):
            Bb, L, H, P = x_multi.shape
            N = Bm.shape[-1]
            dA = jnp.minimum(jnp.exp(dt * A[None, None, :]), 0.99)

            def step(h, inp):
                x_t, B_t, C_t, dA_t = inp
                dBx = jnp.einsum('bhp,bn->bhpn', x_t, B_t)
                h = jnp.clip(dA_t[:, :, None, None] * h + dBx, -10.0, 10.0)
                y_t = jnp.einsum('bn,bhpn->bhp', C_t, h)
                return (h, y_t)
            h0 = jnp.zeros((Bb, H, P, N), dtype=x_multi.dtype)
            xs = (jnp.moveaxis(x_multi, 1, 0), jnp.moveaxis(Bm, 1, 0), jnp.moveaxis(Cm, 1, 0), jnp.moveaxis(dA, 1, 0))
            _, y = jax.lax.scan(step, h0, xs)
            return jnp.moveaxis(y, 0, 1)
        key = jax.random.key(seed)
        ks = jax.random.split(key, 5)
        x = jax.random.normal(ks[0], (BATCH, SEQLEN, D_MODEL), dtype=jnp.float32)
        in_proj_w = jax.random.normal(ks[1], (D_IN_PROJ, D_MODEL), dtype=jnp.float32) * 0.5 * np.sqrt(2.0 / (D_IN_PROJ + D_MODEL))
        out_proj_w = jax.random.normal(ks[2], (D_MODEL, D_INNER), dtype=jnp.float32) * 0.5 * np.sqrt(2.0 / (D_MODEL + D_INNER))
        A_log = jnp.log(jnp.arange(1, NHEADS + 1, dtype=jnp.float32))
        dt_bias = jax.random.normal(ks[3], (NHEADS,), dtype=jnp.float32) * 0.01 + 0.1
        Dparam = jnp.ones((NHEADS,), dtype=jnp.float32)
        return {'x': x, 'in_proj_w': in_proj_w, 'out_proj_w': out_proj_w, 'A_log': A_log, 'dt_bias': dt_bias, 'Dparam': Dparam, 'ln_w': jnp.ones((D_INNER,), jnp.float32), 'ln_b': jnp.zeros((D_INNER,), jnp.float32), 'ni_w': jnp.ones((D_MODEL,), jnp.float32), 'ni_b': jnp.zeros((D_MODEL,), jnp.float32), 'no_w': jnp.ones((D_MODEL,), jnp.float32), 'no_b': jnp.zeros((D_MODEL,), jnp.float32)}
    _L0_attn_in = _L0_attn_setup()

    def _L0_ffn_setup():
        import jax, jax.numpy as jnp
        import numpy as np
        D, H, E, K, S = (128, 256, 8, 2, 1)
        B, L = (4, 256)
        key = jax.random.key(seed)
        ks = jax.random.split(key, 9)
        std = 0.02
        return {'x': jax.random.normal(ks[0], (B, L, D), dtype=jnp.float32), 'router_w': jax.random.normal(ks[1], (E, D), dtype=jnp.float32) * std, 'experts_bias': jnp.zeros((E,), dtype=jnp.float32), 'w1': jax.random.normal(ks[2], (E, D, H), dtype=jnp.float32) * std, 'w3': jax.random.normal(ks[3], (E, D, H), dtype=jnp.float32) * std, 'w2': jax.random.normal(ks[4], (E, H, D), dtype=jnp.float32) * std, 'sw1': jax.random.normal(ks[5], (S, D, H), dtype=jnp.float32) * std, 'sw3': jax.random.normal(ks[6], (S, D, H), dtype=jnp.float32) * std, 'sw2': jax.random.normal(ks[7], (S, H, D), dtype=jnp.float32) * std}
    _L0_ffn_in = _L0_ffn_setup()

    def _L1_attn_setup():
        import jax, jax.numpy as jnp
        import numpy as np
        EMBED_DIM = 128
        NUM_HEADS = 16
        HEAD_DIM = EMBED_DIM // NUM_HEADS
        NUM_DECAYS = 2
        BATCH = 2
        SEQ = 256
        W_SCALE = 0.02
        key = jax.random.key(seed)
        ks = jax.random.split(key, 12)
        d = EMBED_DIM
        inp = {'x': jax.random.normal(ks[0], (BATCH, SEQ, d), dtype=jnp.float32), 'Wq': jax.random.normal(ks[1], (d, d), dtype=jnp.float32) * W_SCALE, 'bq': jnp.zeros((d,), dtype=jnp.float32), 'Wk': jax.random.normal(ks[2], (d, d), dtype=jnp.float32) * W_SCALE, 'bk': jnp.zeros((d,), dtype=jnp.float32), 'Wv': jax.random.normal(ks[3], (d, d), dtype=jnp.float32) * W_SCALE, 'bv': jnp.zeros((d,), dtype=jnp.float32), 'Wo': jax.random.normal(ks[4], (d, d), dtype=jnp.float32) * W_SCALE, 'bo': jnp.zeros((d,), dtype=jnp.float32), 'decay_params': jax.random.uniform(ks[5], (NUM_HEADS, NUM_DECAYS), dtype=jnp.float32), 'mix_weights': jax.random.normal(ks[6], (NUM_HEADS, NUM_DECAYS), dtype=jnp.float32)}
        return inp
    _L1_attn_in = _L1_attn_setup()

    def _L1_ffn_setup():
        import jax, jax.numpy as jnp
        import numpy as np
        B, S, D, O, E, K = (4, 256, 128, 128, 8, 2)
        key = jax.random.key(seed)
        ks = jax.random.split(key, 5)
        scale_in = 1.0 / np.sqrt(D)
        x = jax.random.normal(ks[0], (B, S, D), dtype=jnp.float32)
        gate_w = jax.random.uniform(ks[1], (E, D), jnp.float32, -scale_in, scale_in)
        gate_b = jax.random.uniform(ks[2], (E,), jnp.float32, -scale_in, scale_in)
        expert_w = jax.random.uniform(ks[3], (E, D, O), jnp.float32, -scale_in, scale_in)
        expert_b = jax.random.uniform(ks[4], (E, O), jnp.float32, -scale_in, scale_in)
        return {'x': x, 'gate_w': gate_w, 'gate_b': gate_b, 'expert_w': expert_w, 'expert_b': expert_b}
    _L1_ffn_in = _L1_ffn_setup()
    _d = {'L0_attn_x': _L0_attn_in['x'], 'L0_attn_in_proj_w': _L0_attn_in['in_proj_w'], 'L0_attn_out_proj_w': _L0_attn_in['out_proj_w'], 'L0_attn_A_log': _L0_attn_in['A_log'], 'L0_attn_dt_bias': _L0_attn_in['dt_bias'], 'L0_attn_Dparam': _L0_attn_in['Dparam'], 'L0_attn_ln_w': _L0_attn_in['ln_w'], 'L0_attn_ln_b': _L0_attn_in['ln_b'], 'L0_attn_ni_w': _L0_attn_in['ni_w'], 'L0_attn_ni_b': _L0_attn_in['ni_b'], 'L0_attn_no_w': _L0_attn_in['no_w'], 'L0_attn_no_b': _L0_attn_in['no_b'], 'L0_ffn_router_w': _L0_ffn_in['router_w'], 'L0_ffn_experts_bias': _L0_ffn_in['experts_bias'], 'L0_ffn_w1': _L0_ffn_in['w1'], 'L0_ffn_w3': _L0_ffn_in['w3'], 'L0_ffn_w2': _L0_ffn_in['w2'], 'L0_ffn_sw1': _L0_ffn_in['sw1'], 'L0_ffn_sw3': _L0_ffn_in['sw3'], 'L0_ffn_sw2': _L0_ffn_in['sw2'], 'L1_attn_Wq': _L1_attn_in['Wq'], 'L1_attn_bq': _L1_attn_in['bq'], 'L1_attn_Wk': _L1_attn_in['Wk'], 'L1_attn_bk': _L1_attn_in['bk'], 'L1_attn_Wv': _L1_attn_in['Wv'], 'L1_attn_bv': _L1_attn_in['bv'], 'L1_attn_Wo': _L1_attn_in['Wo'], 'L1_attn_bo': _L1_attn_in['bo'], 'L1_attn_decay_params': _L1_attn_in['decay_params'], 'L1_attn_mix_weights': _L1_attn_in['mix_weights'], 'L1_ffn_gate_w': _L1_ffn_in['gate_w'], 'L1_ffn_gate_b': _L1_ffn_in['gate_b'], 'L1_ffn_expert_w': _L1_ffn_in['expert_w'], 'L1_ffn_expert_b': _L1_ffn_in['expert_b']}
    _x0 = _d['L0_attn_x']
    _d['L0_attn_x'] = jax.random.normal(jax.random.fold_in(jax.random.key(seed), 1), (8, 512, 128), dtype=_x0.dtype)
    del _x0
    return _d

def reference(L0_attn_x, L0_attn_in_proj_w, L0_attn_out_proj_w, L0_attn_A_log, L0_attn_dt_bias, L0_attn_Dparam, L0_attn_ln_w, L0_attn_ln_b, L0_attn_ni_w, L0_attn_ni_b, L0_attn_no_w, L0_attn_no_b, L0_ffn_router_w, L0_ffn_experts_bias, L0_ffn_w1, L0_ffn_w3, L0_ffn_w2, L0_ffn_sw1, L0_ffn_sw3, L0_ffn_sw2, L1_attn_Wq, L1_attn_bq, L1_attn_Wk, L1_attn_bk, L1_attn_Wv, L1_attn_bv, L1_attn_Wo, L1_attn_bo, L1_attn_decay_params, L1_attn_mix_weights, L1_ffn_gate_w, L1_ffn_gate_b, L1_ffn_expert_w, L1_ffn_expert_b):

    def _L0_attn_ref(x, in_proj_w, out_proj_w, A_log, dt_bias, Dparam, ln_w, ln_b, ni_w, ni_b, no_w, no_b):
        import jax, jax.numpy as jnp
        import numpy as np
        D_MODEL = 128
        D_STATE = 64
        HEADDIM = 64
        EXPAND = 2
        D_INNER = D_MODEL * EXPAND
        NHEADS = D_INNER // HEADDIM
        D_IN_PROJ = 2 * D_INNER + 2 * D_STATE + NHEADS
        BATCH, SEQLEN = (4, 512)

        def layernorm(x, w, b, eps=1e-05):
            mu = jnp.mean(x, axis=-1, keepdims=True)
            var = jnp.mean(jnp.square(x - mu), axis=-1, keepdims=True)
            return (x - mu) * jax.lax.rsqrt(var + eps) * w + b

        def _selective_scan(x_multi, A, Bm, Cm, dt):
            Bb, L, H, P = x_multi.shape
            N = Bm.shape[-1]
            dA = jnp.minimum(jnp.exp(dt * A[None, None, :]), 0.99)

            def step(h, inp):
                x_t, B_t, C_t, dA_t = inp
                dBx = jnp.einsum('bhp,bn->bhpn', x_t, B_t)
                h = jnp.clip(dA_t[:, :, None, None] * h + dBx, -10.0, 10.0)
                y_t = jnp.einsum('bn,bhpn->bhp', C_t, h)
                return (h, y_t)
            h0 = jnp.zeros((Bb, H, P, N), dtype=x_multi.dtype)
            xs = (jnp.moveaxis(x_multi, 1, 0), jnp.moveaxis(Bm, 1, 0), jnp.moveaxis(Cm, 1, 0), jnp.moveaxis(dA, 1, 0))
            _, y = jax.lax.scan(step, h0, xs)
            return jnp.moveaxis(y, 0, 1)
        Bb, L, Dm = x.shape
        x_norm = layernorm(x, ni_w, ni_b)
        zxbcdt = jnp.einsum('bld,ed->ble', x_norm, in_proj_w)
        z = zxbcdt[..., :D_INNER]
        x_ssm = zxbcdt[..., D_INNER:2 * D_INNER]
        Bm = zxbcdt[..., 2 * D_INNER:2 * D_INNER + D_STATE]
        Cm = zxbcdt[..., 2 * D_INNER + D_STATE:2 * D_INNER + 2 * D_STATE]
        dt = zxbcdt[..., 2 * D_INNER + 2 * D_STATE:]
        dt = jnp.clip(jax.nn.softplus(dt + dt_bias[None, None, :]), 0.001, 0.1)
        A = -jnp.exp(A_log)
        x_multi = x_ssm.reshape(Bb, L, NHEADS, HEADDIM)
        y = _selective_scan(x_multi, A, Bm, Cm, dt)
        y = y + x_multi * Dparam[None, None, :, None]
        y = y.reshape(Bb, L, D_INNER)
        y = y * jax.nn.silu(z)
        y = layernorm(y, ln_w, ln_b)
        y = jnp.einsum('ble,de->bld', y, out_proj_w)
        y = jnp.clip(y, -10.0, 10.0)
        y = layernorm(y, no_w, no_b)
        return y

    def _L0_ffn_ref(x, router_w, experts_bias, w1, w3, w2, sw1, sw3, sw2):
        import jax, jax.numpy as jnp
        import numpy as np
        D, H, E, K, S = (128, 256, 8, 2, 1)
        B, L = (4, 256)
        b, l, d = x.shape
        xf = x.reshape(-1, d)
        sg = jnp.einsum('td,sdh->tsh', xf, sw1)
        su = jnp.einsum('td,sdh->tsh', xf, sw3)
        shared_out = jnp.einsum('tsh,shd->td', jax.nn.silu(sg) * su, sw2)
        logits = xf @ router_w.T + experts_bias
        rw, sel = jax.lax.top_k(logits, K)
        rw = jax.nn.softmax(rw.astype(jnp.float32), axis=-1).astype(x.dtype)
        cw = (jax.nn.one_hot(sel, E, dtype=x.dtype) * rw[..., None]).sum(axis=1)
        g = jnp.einsum('td,edh->teh', xf, w1)
        u = jnp.einsum('td,edh->teh', xf, w3)
        eo = jax.nn.silu(g) * u
        moe_out = jnp.einsum('te,teh,ehd->td', cw, eo, w2)
        return (moe_out + shared_out).reshape(b, l, d)

    def _L1_attn_ref(x, Wq, bq, Wk, bk, Wv, bv, Wo, bo, decay_params, mix_weights):
        import jax, jax.numpy as jnp
        import numpy as np
        EMBED_DIM = 128
        NUM_HEADS = 16
        HEAD_DIM = EMBED_DIM // NUM_HEADS
        NUM_DECAYS = 2
        BATCH = 2
        SEQ = 256
        W_SCALE = 0.02
        B, S, _ = x.shape
        H, D = (NUM_HEADS, HEAD_DIM)

        def proj(W, b):
            return (jnp.einsum('bse,fe->bsf', x, W) + b).reshape(B, S, H, D).transpose(0, 2, 1, 3)
        q = proj(Wq, bq)
        k = proj(Wk, bk)
        v = proj(Wv, bv)
        attn_scores = jnp.einsum('bhqd,bhkd->bhqk', q, k) / jnp.sqrt(jnp.float32(D))
        t = jnp.arange(S, dtype=jnp.float32)
        time_diffs = jnp.abs(t[:, None] - t[None, :])
        dp = jnp.clip(decay_params, 0.01, 0.9999)
        decay_masks = dp[:, :, None, None] ** time_diffs[None, None, :, :]
        mix = jax.nn.softmax(mix_weights, axis=-1)
        decay_mask = jnp.einsum('hnqk,hn->hqk', decay_masks, mix)
        attn_scores = attn_scores * decay_mask[None]
        attn_probs = jax.nn.softmax(attn_scores, axis=-1)
        out = jnp.einsum('bhqk,bhkd->bhqd', attn_probs, v)
        out = out.transpose(0, 2, 1, 3).reshape(B, S, H * D)
        return jnp.einsum('bse,fe->bsf', out, Wo) + bo

    def _L1_ffn_ref(x, gate_w, gate_b, expert_w, expert_b):
        import jax, jax.numpy as jnp
        import numpy as np
        B, S, D, O, E, K = (4, 256, 128, 128, 8, 2)
        logits = jnp.einsum('bsd,ed->bse', x, gate_w) + gate_b
        if K < E:
            topv, topi = jax.lax.top_k(logits, K)
            keep = jax.nn.one_hot(topi, E, dtype=jnp.float32).sum(axis=-2)
            logits = jnp.where(keep > 0, logits, -jnp.inf)
        gate_score = jax.nn.softmax(logits, axis=-1)
        expert_out = jnp.einsum('bsd,edo->bseo', x, expert_w) + expert_b
        out = jnp.einsum('bseo,bse->bso', expert_out, gate_score)
        return out
    x = L0_attn_x
    xn = _layernorm(x, axis=-1)
    x = x + _L0_attn_ref(xn, L0_attn_in_proj_w, L0_attn_out_proj_w, L0_attn_A_log, L0_attn_dt_bias, L0_attn_Dparam, L0_attn_ln_w, L0_attn_ln_b, L0_attn_ni_w, L0_attn_ni_b, L0_attn_no_w, L0_attn_no_b) + _L0_ffn_ref(xn, L0_ffn_router_w, L0_ffn_experts_bias, L0_ffn_w1, L0_ffn_w3, L0_ffn_w2, L0_ffn_sw1, L0_ffn_sw3, L0_ffn_sw2)
    xn = _layernorm(x, axis=-1)
    x = x + _L1_attn_ref(xn, L1_attn_Wq, L1_attn_bq, L1_attn_Wk, L1_attn_bk, L1_attn_Wv, L1_attn_bv, L1_attn_Wo, L1_attn_bo, L1_attn_decay_params, L1_attn_mix_weights) + _L1_ffn_ref(xn, L1_ffn_gate_w, L1_ffn_gate_b, L1_ffn_expert_w, L1_ffn_expert_b)
    return x

_drawn_inputs = setup_inputs


def setup_inputs(seed=0):
    import zlib

    import numpy as np

    out = dict(_drawn_inputs(seed))
    spreads = {'L0_attn_Dparam': (1.0, 0.2),
     'L0_attn_ln_w': (1.0, 0.2),
     'L0_attn_ln_b': (0.0, 0.1),
     'L0_attn_ni_w': (1.0, 0.2),
     'L0_attn_ni_b': (0.0, 0.1),
     'L0_attn_no_w': (1.0, 0.2),
     'L0_attn_no_b': (0.0, 0.1),
     'L0_ffn_experts_bias': (0.0, 0.8),
     'L1_attn_bq': (0.0, 0.8),
     'L1_attn_bk': (0.0, 2.0),
     'L1_attn_bv': (0.0, 0.511),
     'L1_attn_bo': (0.0, 0.1)}
    factors = {'L0_ffn_router_w': 4.536,
     'L0_ffn_w1': 3.539,
     'L0_ffn_w3': 3.925,
     'L0_ffn_w2': 3.777,
     'L0_ffn_sw1': 3.233,
     'L0_ffn_sw3': 3.173,
     'L0_ffn_sw2': 2.911,
     'L1_attn_Wq': 8.0,
     'L1_attn_Wk': 8.0,
     'L1_attn_Wv': 8.0,
     'L1_attn_Wo': 3.364,
     'L1_attn_decay_params': 8.0,
     'L1_attn_mix_weights': 8.0,
     'L1_ffn_expert_b': 2.764}
    for name, (base, spread) in spreads.items():
        noise = np.random.default_rng([zlib.crc32(name.encode()), seed]).standard_normal(out[name].shape)
        drawn = base * np.exp(spread * noise) if base else spread * noise
        out[name] = jnp.asarray(drawn.astype(out[name].dtype))
    for name, factor in factors.items():
        out[name] = (out[name] * factor).astype(out[name].dtype)
    return out
```

```python
import math
from contextlib import ExitStack

import concourse.bass as bass
from concourse import mybir

F32 = mybir.dt.float32
F16 = mybir.dt.float16
BF16 = mybir.dt.bfloat16
I32 = mybir.dt.int32
ALU = mybir.AluOpType
ACT = mybir.ActivationFunctionType
AX = mybir.AxisListType.X

P = 128
NB, S, DM = 8, 512, 128
NT = S // P
TT = NB * NT
NH, HD = 4, 64
DI = NH * HD
NS = 64
E, FH = 8, 256
AH, AD = 16, 8
EPS = 1e-5
LOG_MAX_DECAY = math.log(0.99)
CLIP = 10.0
SAFE = 0.99 * CLIP * CLIP
MASKED = -1e30


DVE_A = 74


DVE_B = 34
DVE_C = 102
WTS_C = 19
MW = 896


class Chain:

    def __init__(self, eng, sem):
        self.eng, self.sem, self.base, self.n = eng, sem, 0, 0

    def did(self, ins):
        ins.then_inc(self.sem, 1)
        self.n += 1
        return self.n

    def after(self, k):
        self.eng.wait_ge(self.sem, self.base + k)

    def now(self, ins):
        self.after(self.did(ins))


class Norm:

    def __init__(self, sb, name):
        t = lambda n, *shape: sb(f"{name}_{n}", [P, NT, *shape])
        self.stats, self.mv, self.var, self.ln, self.rs, self.t, self.rstd = (
            t("stats", 6), t("mv", 2), t("var"), t("ln"), t("rs"), t("t"), t("rstd"))


def rsqrt_by_exp(nc, act, own, nm, var_ok, rs_ok, turn):
    act.wait_ge(var_ok, turn)
    own.now(nc.scalar.activation(nm.ln[:], nm.var[:], ACT.Ln))
    nc.scalar.activation(nm.rs[:], nm.ln[:], ACT.Exp, scale=-0.5).then_inc(rs_ok, 1)


def normed(nc, dve, own, gap, nm, src, dst, var_ok, rs_ok, turn):
    dve.sem_inc(gap, 1)
    for t in range(NT):
        i = own.did(nc.vector.bn_stats(nm.stats[:, t], src(t)))
    own.after(i)
    dve.sem_inc(gap, 1)
    for t in range(NT):
        i = own.did(nc.vector.bn_aggr(nm.mv[:, t], nm.stats[:, t]))
    own.after(i)
    nc.vector.tensor_scalar(nm.var[:], nm.mv[:, :, 1], EPS, None, ALU.add).then_inc(var_ok, 1)
    dve.wait_ge(rs_ok, turn)
    own.now(nc.vector.tensor_tensor(nm.t[:], nm.rs[:], nm.var[:], ALU.mult))
    own.now(nc.vector.tensor_tensor(nm.t[:], nm.t[:], nm.rs[:], ALU.mult))
    own.now(nc.vector.tensor_scalar(nm.t[:], nm.t[:], -0.5, 1.5, ALU.mult, ALU.add))
    own.now(nc.vector.tensor_tensor(nm.rstd[:], nm.t[:], nm.rs[:], ALU.mult))
    for t in range(NT):
        i = own.did(nc.vector.tensor_scalar(dst[:, t], src(t), nm.mv[:, t, 0:1], nm.rstd[:, t:t + 1],
                                            ALU.subtract, ALU.mult))
    own.after(i)


class Router:

    def __init__(self, sb, name):
        t = lambda n, *shape: sb(f"{name}_{n}", [P, NT, *shape])
        self.lg, self.m8, self.masked_out, self.rep = t("lg", E), t("m8", 8), t("kill", 8), t("rep", E)
        self.sh, self.ex, self.sum, self.inv = t("sh", E), t("ex", E), t("sum"), t("inv")


def choose_two(nc, dve, own, gap, rt, logits, bias, read_ok, shifted_ok, exp_ok, turn, weights):
    nc.vector.tensor_tensor(rt.lg[:], logits, bias[:].unsqueeze(1).broadcast_to([P, NT, E]), ALU.add).then_inc(read_ok, 1)
    dve.wait_ge(read_ok, turn)
    dve.sem_inc(gap, 1)
    for t in range(NT):
        i = own.did(nc.vector.max(rt.m8[:, t], rt.lg[:, t]))
    own.after(i)
    nc.vector.tensor_tensor(rt.sh[:], rt.lg[:], rt.m8[:, :, 0:1].broadcast_to([P, NT, E]), ALU.subtract).then_inc(shifted_ok, 1)
    own.now(nc.vector.tensor_copy(rt.masked_out[:, :, 0:2], rt.m8[:, :, 0:2]))
    dve.sem_inc(gap, 1)
    for t in range(NT):
        i = own.did(nc.vector.match_replace(rt.rep[:, t], rt.masked_out[:, t], rt.lg[:, t], MASKED))
    own.after(i)
    own.now(nc.vector.tensor_tensor(rt.rep[:], rt.rep[:], rt.lg[:], ALU.not_equal))
    dve.wait_ge(exp_ok, turn)
    own.now(nc.vector.tensor_tensor(rt.ex[:], rt.ex[:], rt.rep[:], ALU.mult))
    own.now(nc.vector.tensor_reduce(rt.sum[:], rt.ex[:], AX, ALU.add))
    own.now(nc.vector.reciprocal(rt.inv[:], rt.sum[:]))
    return own.did(nc.vector.tensor_tensor(weights, rt.ex[:], rt.inv[:].unsqueeze(2).broadcast_to([P, NT, E]), ALU.mult))


def two_layers_kernel(nc, ins, out):
    ctx = ExitStack()
    with ctx:
        def sb(name, shape, dt=F32):
            return ctx.enter_context(nc.sbuf_tensor(name, shape, dt))

        def in_scope(stack):
            return lambda name, shape, dt=F32: stack.enter_context(nc.sbuf_tensor(name, shape, dt))

        def dram(name, shape, dt=F32):
            return nc.dram_tensor(name, shape, dt, kind="Internal").ap()

        def sem(name):
            return ctx.enter_context(nc.semaphore(name))

        def row_on_all(ap, n):
            return bass.AP(tensor=ap.tensor, offset=ap.offset, ap=[[0, P], [1, n]])

        x1 = sb("x1", [P, TT, DM])
        y_all = sb("y_all", [P, TT, DI])
        ident = sb("ident", [P, P])
        ident_b = sb("ident_b", [P, P], BF16)
        peak = sb("peak", [P, NB, 2, NT * 2])
        wo = sb("wo", [P, 2, DM])
        ln_cols = sb("ln_cols", [P, 2, 2])
        no_rows = sb("no_rows", [P, 2, DM])
        wqkv = sb("wqkv", [P, 3, DM])
        w_att = sb("w_att", [P, DM])
        bqk = sb("bqk", [P, 2])
        bv_row = sb("bv_row", [P, DM])
        bo_row = sb("bo_row", [P, DM])
        gate_w = sb("gate_w", [P, E])
        gate_b = sb("gate_b", [P, E])
        ew = sb("ew", [P, E, DM])
        eb = sb("eb", [E, DM])
        dp = sb("dp", [AH, 2])
        mix = sb("mix", [AH, 2])
        early = ctx.enter_context(ExitStack())
        sb_early = in_scope(early)
        xnT = sb_early("xnT", [P, NB, S])
        z_all = sb_early("z_all", [P, TT, DI])
        w13 = sb_early("w13", [P, 1 + E, 2, FH])
        w2 = sb_early("w2", [P, 1 + E, 2, DM])
        cw_all = sb_early("cw_all", [P, TT, E])
        router_w = sb_early("router_w", [P, E])
        router_b = sb_early("router_b", [P, E])
        w_zx = sb_early("w_zx", [P, 2 * DI])
        w_bcd = sb_early("w_bcd", [P, 2 * NS + NH])
        w_bb = sb_early("w_bb", [P, 2, NS])
        w_cc = sb_early("w_cc", [P, 2, NS])
        ni = sb_early("ni", [P, 2])
        head_rows = sb_early("head_rows", [P, 3, NH])
        neg_a = sb_early("neg_a", [P, NH])
        upper = sb_early("upper", [P, P])
        ones = sb_early("ones", [P, P])
        strict_b = sb_early("strict_b", [P, P], BF16)
        d_row = sb_early("d_row", [P, NH, HD])

        xT_d = dram("xT_d", (NB, P, 2, S))
        dec_d = dram("dec_d", (NB, P, 2, S))
        bc_d = dram("bc_d", (NB, NT, P, 2 * NS))
        mirror_d = dram("mirror_d", (AH, 2 * S))
        parts_d = dram("parts_d", (2, 3, NB, P, S), BF16)
        mirrored, wts_c, mask_in, mix_ex = sem("mirrored"), sem("wts_c"), sem("mask_in"), sem("mix_ex")

        banks = [ctx.enter_context(nc.psum_tensor(f"bank{i}", [P, 512], F32)) for i in range(8)]

        x_first, x_rest, wts, wts_b = sem("x_first"), sem("x_rest"), sem("wts"), sem("wts_b")
        consts = sem("consts")
        dve_own, act_own, pool_own = sem("dve_own"), sem("act_own"), sem("pool_own")
        var1, var2, rs1, rs2 = sem("var1"), sem("var2"), sem("rs1"), sem("rs2")
        stats_ok, xn_ok, xh_ok = sem('stats_ok'), sem("xn_ok"), sem("xh_ok")
        xnT_ps, xhT_ps, xnT_ok, xhT_ok = sem("xnT_ps"), sem("xhT_ps"), sem("xnT_ok"), sem("xhT_ok")
        zx_ps, zx_ok, bcd_ps, bcd_ok = sem("zx_ps"), sem("zx_ok"), sem("bcd_ps"), sem("bcd_ok")
        em_ps, em_ok = sem("em_ps"), sem("em_ok")
        dt_v, dt_e, dt_u, dt_l, dt_w_ok, dt_x = (sem(n) for n in ("dt_v", "dt_e", "dt_u", "dt_l", "dt_w_ok", "dt_x"))
        la_ok, decay_ok, cum_ps, ect_ok, ncum_ok, etail_ok = (
            sem(n) for n in ("la_ok", "decay_ok", "cum_ps", "ect_ok", "ncum_ok", "etail_ok"))
        dbc_ps, dbc_ok, dbc_used = sem("dbc_ps"), sem("dbc_ok"), sem("dbc_used")
        g_ps, l_ps, l_ok, m_ok, xw_ok, xd_ok = (sem(n) for n in ("g_ps", "l_ps", "l_ok", "m_ok", "xw_ok", "xd_ok"))
        y_ps, y_ok, h_ps, h_ok = sem("y_ps"), sem("y_ok"), sem("h_ps"), sem("h_ok")
        spilled = sem("spilled")
        xnc_ps, rt_ps, rt_sh, rt_ex, rt_done = (sem(n) for n in ("xnc_ps", "rt_ps", "rt_sh", "rt_ex", "rt_done"))
        scan_ok, scT_ps, pk_ok, xnT_all = sem("scan_ok"), sem("scT_ps"), sem("pk_ok"), sem("xnT_all")

        x_v = ins["x"].rearrange("b (t p) d -> p b t d", p=P)

        with ExitStack() as work:
            wb = in_scope(work)
            nm1, nm2 = Norm(wb, "nm1"), Norm(wb, "nm2")
            mix_w = wb("mix_w", [AH, 8])
            table_ok = sem("table_ok")
            xn = wb("xn", [P, NT, DM])
            xh = wb("xh", [P, NT, DM])
            xhT = wb("xhT", [P, S])
            xs = wb("xs", [P, NT, DI])
            bcd = wb("bcd", [P, NT, 2 * NS + NH])
            xT = wb("xT", [P, 2, S])
            xT2 = wb("xT2", [P, 2, S])
            bT = wb("bT", [P, S])
            bT2 = wb("bT2", [P, S])
            cT = wb("cT", [P, S])
            dt_w = wb("dt_w", [P, 12, NT, NH])
            decay = wb("decay", [P, NT, NH])
            la = wb("la", [P, NT, NH])
            ncum = wb("ncum", [P, NT, NH])
            tail = wb("tail", [P, NT, NH])
            e_ct = wb("e_ct", [P, 2, NT, NH])
            e_tail = wb("e_tail", [P, NT, NH])
            lmat = wb("lmat", [P, 2, NH, P])
            mt = wb("mt", [P, 2, NH, P])
            xw = wb("xw", [P, NT, NH, HD])
            xd = wb("xd", [P, NT, NH, HD])
            powers = xw[0:AH].rearrange("p t h d -> p (t h d)").rearrange("p (n s) -> p n s", n=2)
            table = xd[0:AH, 0:2].rearrange("p t h d -> p (t h d)")
            table_r = xd[0:AH, 2:4].rearrange("p t h d -> p (t h d)")
            yt = wb("yt", [P, 2, DI])
            state = wb("state", [P, DI])
            scan_out = wb("scan_out", [P, 4, S])
            dec_bc = wb("dec_bc", [P, 2, S])
            xnc = wb("xnc", [P, S])
            tops = wb("tops", [P, 4, NT])
            pk = wb("pk", [P, 4, NT * 2])
            rt = Router(wb, "rt")


            block = work.enter_context(nc.Block())

            @block.sync
            def _(sp):
                x1v = x1[:].rearrange("p (b t) d -> p b t d", b=NB)
                sp.dma_start(x1v[:, 0], x_v[:, 0]).then_inc(x_first, 16)
                sp.dma_start(ident[:], ins["ident"]).then_inc(wts, 16)
                sp.dma_start(ni[:, 0:1], ins["ni_w"].rearrange("(p a) -> p a", a=1)).then_inc(wts, 16)
                sp.dma_start(ni[:, 1:2], ins["ni_b"].rearrange("(p a) -> p a", a=1)).then_inc(wts, 16)
                sp.dma_start(w_zx[:], ins["in_wT"][:, 0:2 * DI]).then_inc(wts, 16)
                sp.dma_start(w_bcd[:], ins["in_wT"][:, 2 * DI:]).then_inc(wts, 16)
                for j in range(2):
                    sp.dma_start(w_bb[:, j], ins["in_wT"][:, 2 * DI:2 * DI + NS]).then_inc(wts, 16)
                    sp.dma_start(w_cc[:, j], ins["in_wT"][:, 2 * DI + NS:2 * DI + 2 * NS]).then_inc(wts, 16)
                for j, n in enumerate(("A_log", "dt_bias", "Dparam")):
                    sp.dma_start(head_rows[:, j], row_on_all(ins[n], NH)).then_inc(wts, 16)
                sp.dma_start(router_w[:], ins["router_wT"]).then_inc(wts, 16)
                sp.dma_start(router_b[:], row_on_all(ins["experts_bias"], E)).then_inc(wts, 16)
                sp.dma_start(x1v[:, 1:], x_v[:, 1:]).then_inc(x_rest, 16)
                for m in range(2):
                    sp.dma_start(w13[:, 0, m], ins[("sw1", "sw3")[m]][0]).then_inc(wts_b, 16)
                    sp.dma_start(w13[:, 1:, m], ins[("w1", "w3")[m]].rearrange("e d h -> d e h")).then_inc(wts_b, 16)
                    sp.dma_start(w2[:, 0, m], ins["sw2"][0, m * P:(m + 1) * P]).then_inc(wts_b, 16)
                    sp.dma_start(w2[:, 1:, m], ins["w2"][:, m * P:(m + 1) * P].rearrange("e h d -> h e d")).then_inc(wts_b, 16)
                load = lambda dst, src: sp.dma_start(dst, src).then_inc(wts_c, 16)
                load(dp[:], ins["decay_params"])
                load(mix[:], ins["mix_weights"])
                load(wo[:], ins["out_wT"].rearrange("(j p) d -> p j d", p=P))
                load(ln_cols[:, 0], ins["ln_w"])
                load(ln_cols[:, 1], ins["ln_b"])
                load(no_rows[:, 0], row_on_all(ins["no_w"], DM))
                load(no_rows[:, 1], row_on_all(ins["no_b"], DM))
                for j, n in enumerate("qkv"):
                    load(wqkv[:, j], ins[f"w{n}T"])
                load(w_att[:], ins["woT"])
                load(bqk[:, 0:1], ins["bq"])
                load(bqk[:, 1:2], ins["bk"])
                load(bv_row[:], row_on_all(ins["bv"], DM))
                load(bo_row[:], row_on_all(ins["bo"], DM))
                load(gate_w[:], ins["gate_wT"])
                load(gate_b[:], row_on_all(ins["gate_b"], E))
                load(ew[:], ins["expert_w"].rearrange("e d o -> d e o"))
                load(eb[:], ins["expert_b"])
                sp.wait_ge(table_ok, 2)
                sp.dma_start(mirror_d[:, S - 1:2 * S - 1], table[:]).then_inc(mirrored, 16)
                sp.dma_start(mirror_d[:, 0:S - 1], table_r[:, 0:S - 1]).then_inc(mirrored, 16)
                sp.sem_inc(spilled, 16)
                with sp.Fori(0, NB) as b:
                    sp.wait_ge(bcd_ok, b * NT + NT)
                    sp.dma_start(bc_d[bass.ds(b, 1)].rearrange("a t p n -> p (a t) n"),
                                 bcd[:, :, 0:2 * NS]).then_inc(spilled, 16)
                    sp.wait_ge(em_ok, b * 7 + 2)
                    sp.dma_start(xT_d[bass.ds(b, 1)].rearrange("a p h s -> p (a h) s"), xT[:]).then_inc(spilled, 16)
                    sp.wait_ge(dbc_ok, b * 2 + 2)
                    sp.dma_start(dec_d[bass.ds(b, 1)].rearrange("a p h s -> p (a h) s"), dec_bc[:]).then_inc(spilled, 16)
                sp.wait_ge(spilled, 16 + 48 * NB)

            @block.gpsimd
            def _(pool):
                own = Chain(pool, pool_own)
                own.now(nc.gpsimd.memset(ones[:], 1.0))
                own.now(nc.gpsimd.affine_select(out=upper[:], in_=ones[:], compare_op=ALU.is_ge, fill=0.0, base=0,
                                                pattern=[[1, P]], channel_multiplier=-1))
                nc.gpsimd.memset(state[:], 0.0).then_inc(consts, 1)
                own.now(nc.gpsimd.memset(strict_b[:], 0.0))
                nc.gpsimd.affine_select(out=strict_b[:], in_=strict_b[:], compare_op=ALU.is_ge, fill=MASKED, base=0,
                                        pattern=[[1, P]], channel_multiplier=-1).then_inc(consts, 1)
                pool.wait_ge(wts, 16 * 14)
                nc.gpsimd.tensor_copy(ident_b[:], ident[:]).then_inc(consts, 1)
                own.now(nc.gpsimd.tensor_copy(d_row[:], head_rows[:, 2].unsqueeze(2).broadcast_to([P, NH, HD])))
                pool.wait_ge(mirrored, 32)
                pool.sem_inc(xnT_all, 1)
                with pool.Fori(0, NB) as b:
                    pool.wait_ge(xnT_ok, b + 1)
                    nc.gpsimd.tensor_copy(xnT[:, bass.ds(b, 1)].rearrange("p a s -> p (a s)"), xnc[:]).then_inc(xnT_all, 1)
                    pool.wait_ge(zx_ok, b * 2 * NT + 2 * NT)
                    for t in range(NT):
                        if t == 0:
                            pool.wait_ge(y_ok, b * NT + 1)
                        nc.gpsimd.tensor_tensor(xd[:, t], xs[:, t].rearrange("p (h d) -> p h d", h=NH), d_row[:],
                                                ALU.mult).then_inc(xd_ok, 1)
                    pool.wait_ge(etail_ok, b + 1)
                    for t in range(NT - 1):
                        nc.gpsimd.tensor_tensor(xw[:, t], xs[:, t].rearrange("p (h d) -> p h d", h=NH),
                                                e_tail[:, t].unsqueeze(2).broadcast_to([P, NH, HD]),
                                                ALU.mult).then_inc(xw_ok, 1)

            @block.tensor
            def _(pe):
                pe.wait_ge(wts, 16 * 14)
                pe.wait_ge(consts, 3)
                with pe.Fori(0, NB) as b:
                    pe.wait_ge(xn_ok, b + 1)
                    for t in range(NT):
                        i = pe.transpose(banks[0][:, t * P:(t + 1) * P], xn[:, t], ident[:])
                    i.then_inc(xnT_ps, 1)
                    pe.wait_ge(xh_ok, b + 1)
                    for t in range(NT):
                        i = pe.transpose(banks[1][:, t * P:(t + 1) * P], xh[:, t], ident[:])
                    i.then_inc(xhT_ps, 1)
                    pe.wait_ge(xhT_ok, b + 1)
                    for t in range(NT):
                        lhsT = xhT[:, t * P:(t + 1) * P]
                        if t < 2:
                            pe.wait_ge(pk_ok, b * 4 + 1 + 2 + t)
                        else:
                            pe.wait_ge(zx_ok, b * 2 * NT + 2 * (t - 1))
                            pe.wait_ge(bcd_ok, b * NT + t - 1)
                        pe.matmul(banks[2 + t % 2][:], lhsT, w_zx[:], start=True, stop=True).then_inc(zx_ps, 1)
                        pe.matmul(banks[4 + t % 2][:, 0:2 * NS + NH], lhsT, w_bcd[:], start=True, stop=True).then_inc(bcd_ps, 1)
                    pe.wait_ge(xnT_ok, b + 1)
                    for t in range(NT):
                        i = pe.matmul(banks[6][:, t * E:(t + 1) * E], xnc[:, t * P:(t + 1) * P], router_w[:], start=True, stop=True)
                    i.then_inc(rt_ps, 1)
                    pe.wait_ge(xnT_ok, b + 1)
                    for j, (w, k) in enumerate(((w_zx[:, DI:DI + P], 0), (w_zx[:, DI + P:], 1),
                                                (w_bb[:].rearrange("p a n -> p (a n)"), 6),
                                                (w_cc[:].rearrange("p a n -> p (a n)"), 7))):
                        if k == 6:
                            pe.wait_ge(rt_done, b + 1)
                        pe.matmul(banks[k][:], w, xhT[:], start=True, stop=True).then_inc(em_ps, 1)
                    pe.wait_ge(la_ok, b + 1)
                    lav = la[:].rearrange("p t h -> p (t h)")
                    pe.matmul(banks[4][:, 0:NT * NH], upper[:], lav, start=True, stop=True)
                    pe.matmul(banks[4][:, NT * NH:2 * NT * NH], ones[:], lav, start=False, stop=True,
                              skip_group_check=True).then_inc(cum_ps, 1)
                    pe.wait_ge(zx_ok, b * 2 * NT + 2 * NT)
                    pe.wait_ge(decay_ok, b + 1)
                    for half in range(2):
                        for t in range(NT):
                            for j in range(2):
                                h = 2 * half + j
                                i = pe.matmul(banks[2 + half][HD * j:HD * (j + 1), t * P:(t + 1) * P],
                                              decay[:, t, h:h + 1].broadcast_to([P, HD]), ident[:],
                                              start=(t == 0), stop=True, skip_group_check=True)
                        i.then_inc(dbc_ps, 1)
                    pe.wait_ge(em_ok, b * 7 + 7)
                    pe.wait_ge(bcd_ok, b * NT + NT)
                    for t in range(NT):
                        i = pe.matmul(banks[5][:, t * P:(t + 1) * P], bT[:, t * P:(t + 1) * P], cT[:, t * P:(t + 1) * P],
                                      start=(t == 0), stop=True, skip_group_check=True)
                    i.then_inc(g_ps, 1)

                    def decays(c):
                        k = banks[c % 2]
                        if c >= 2:
                            pe.wait_ge(l_ok, b * NT + c - 1)
                        pe.matmul(k[:], ident_b[:], strict_b[:].unsqueeze(1).broadcast_to([P, NH, P]),
                                  start=True, stop=True, skip_group_check=True)
                        for h in range(NH):
                            i = pe.matmul(k[:, h * P:(h + 1) * P], la[:, c, h:h + 1].broadcast_to([P, P]), upper[:],
                                          start=False, stop=True, skip_group_check=True)
                        i.then_inc(l_ps, 1)

                    decays(0)
                    decays(1)
                    for c in range(NT):
                        if c + 2 < NT:
                            decays(c + 2)
                        yb, hb = banks[6 + c % 2], banks[4]
                        pe.wait_ge(m_ok, b * NT + c + 1)
                        if c >= 2:
                            pe.wait_ge(y_ok, b * NT + c)
                        for h in range(NH):
                            i = pe.matmul(yb[:, h * HD:(h + 1) * HD], mt[:, c % 2, h], xs[:, c, h * HD:(h + 1) * HD],
                                          start=(h == 0), stop=True, skip_group_check=True)
                        if c:
                            pe.wait_ge(h_ok, b * (NT - 1) + c)
                            i = pe.matmul(yb[:, DI:2 * DI], cT[:, c * P:(c + 1) * P], state[:], start=False, stop=True,
                                          skip_group_check=True)
                        i.then_inc(y_ps, 1)
                        if c < NT - 1:
                            if c == 0:
                                pe.wait_ge(ncum_ok, b + 1)
                                pe.wait_ge(ect_ok, b + 1)
                            pe.wait_ge(xw_ok, b * (NT - 1) + c + 1)
                            for j in range(2):
                                i = pe.matmul(hb[NS * j:NS * (j + 1), 0:DI], bcd[:, c, 0:NS],
                                              xw[:, c].rearrange("p h d -> p (h d)"), start=True, stop=True)
                            i.then_inc(h_ps, 1)
                    for k in range(4):
                        pe.wait_ge(scan_ok, b * 4 + k + 1)
                        pe.wait_ge(dbc_ok, b * 2 + 2)
                        if k >= 2:
                            pe.wait_ge(pk_ok, b * 4 + 4 + k - 1)
                        for t in range(NT):
                            i = pe.transpose(banks[2 + k % 2][:, t * P:(t + 1) * P], scan_out[:, k, t * P:(t + 1) * P], ident[:])
                        i.then_inc(scT_ps, 1)

            @block.scalar
            def _(act):
                own = Chain(act, act_own)
                act.wait_ge(wts, 16 * 14)
                own.now(nc.scalar.activation(neg_a[:], head_rows[:, 0], ACT.Exp))
                own.now(nc.scalar.mul(neg_a[:], neg_a[:], -1.0))
                act.wait_ge(mix_ex, 1)
                nc.scalar.activation(mix_w[:, 4:6], mix_w[:, 2:4], ACT.Exp).then_inc(mix_ex, 1)
                first = own.n
                nc.scalar.preload_act_table_set("natural_log_exp_and_others")

                with act.Fori(0, NB) as b:
                    own.base, own.n = b * 2 + first, 0
                    rsqrt_by_exp(nc, act, own, nm1, var1, rs1, b + 1)
                    rsqrt_by_exp(nc, act, own, nm2, var2, rs2, b + 1)
                    act.wait_ge(xnT_ps, b + 1)
                    act.wait_ge(xnT_all, b + 1)
                    nc.scalar.copy(xnc[:], banks[0][:]).then_inc(xnT_ok, 1)
                    act.wait_ge(xhT_ps, b + 1)
                    nc.scalar.activation(xhT[:], banks[1][:], ACT.Identity, scale=ni[:, 0:1], bias=ni[:, 1:2]).then_inc(xhT_ok, 1)
                    for t in range(NT):
                        act.wait_ge(zx_ps, b * NT + t + 1)
                        nc.scalar.copy(z_all[:, bass.ds(b * NT + t, 1)].rearrange("p a d -> p (a d)"),
                                       banks[2 + t % 2][:, 0:DI]).then_inc(zx_ok, 1)
                        nc.scalar.copy(xs[:, t], banks[2 + t % 2][:, DI:]).then_inc(zx_ok, 1)
                        act.wait_ge(bcd_ps, b * NT + t + 1)
                        if t == 0:
                            act.wait_ge(spilled, b * 48 + 16)
                        nc.scalar.copy(bcd[:, t], banks[4 + t % 2][:, 0:2 * NS + NH]).then_inc(bcd_ok, 1)
                    for j, k in ((0, 0), (1, 1)):
                        act.wait_ge(em_ps, b * 4 + j + 1)
                        nc.scalar.copy(xT[:, j], banks[k][:]).then_inc(em_ok, 1)
                    for j, k in ((0, 0), (1, 1)):
                        nc.scalar.activation(xT2[:, j], banks[k][:], ACT.Square).then_inc(em_ok, 1)
                    act.wait_ge(em_ps, b * 4 + 3)
                    nc.scalar.copy(bT[:], banks[6][:]).then_inc(em_ok, 1)
                    nc.scalar.activation(bT2[:], banks[6][:], ACT.Square).then_inc(em_ok, 1)
                    act.wait_ge(em_ps, b * 4 + 4)
                    nc.scalar.copy(cT[:], banks[7][:]).then_inc(em_ok, 1)
                    act.wait_ge(rt_sh, b + 1)
                    nc.scalar.activation(rt.ex[:], rt.sh[:], ACT.Exp).then_inc(rt_ex, 1)
                    act.wait_ge(dt_v, b + 1)
                    nc.scalar.activation(dt_w[:, 1], dt_w[:, 0], ACT.Exp).then_inc(dt_e, 1)
                    act.wait_ge(dt_u, b + 1)
                    nc.scalar.activation(dt_w[:, 3], dt_w[:, 2], ACT.Ln).then_inc(dt_l, 1)
                    act.wait_ge(dt_w_ok, b + 1)
                    nc.scalar.activation(dt_w[:, 9], dt_w[:, 8], ACT.Exp).then_inc(dt_x, 1)
                    act.wait_ge(cum_ps, b + 1)
                    nc.scalar.activation(e_ct[:].rearrange("p a t h -> p (a t h)"), banks[4][:, 0:2 * NT * NH],
                                         ACT.Exp).then_inc(ect_ok, 1)
                    act.wait_ge(ncum_ok, b + 1)
                    nc.scalar.activation(e_tail[:], tail[:], ACT.Exp).then_inc(etail_ok, 1)
                    for half in range(2):
                        act.wait_ge(dbc_ps, b * 2 + half + 1)
                        nc.scalar.copy(dec_bc[:, half], banks[2 + half][:]).then_inc(dbc_ok, 1)
                    for c in range(NT):
                        act.wait_ge(l_ps, b * NT + c + 1)
                        if c >= 2:
                            act.wait_ge(m_ok, b * NT + c - 1)
                        for h in range(NH):
                            i = nc.scalar.activation(lmat[:, c % 2, h], banks[c % 2][:, h * P:(h + 1) * P], ACT.Exp,
                                                     bias=ncum[:, c, h:h + 1])
                        i.then_inc(l_ok, 1)
                    assert own.n == 2

            @block.vector
            def _(dve):
                own = Chain(dve, dve_own)
                dve.wait_ge(wts_c, 16 * WTS_C)
                own.now(nc.vector.tensor_scalar(dp[:], dp[:], 0.01, 0.9999, ALU.max, ALU.min))
                own.now(nc.vector.tensor_reduce(mix_w[:, 0:1], mix[:], AX, ALU.max))
                nc.vector.tensor_scalar(mix_w[:, 2:4], mix[:], mix_w[:, 0:1], None, ALU.subtract).then_inc(mix_ex, 1)
                dve.wait_ge(mix_ex, 2)
                own.now(nc.vector.tensor_reduce(mix_w[:, 1:2], mix_w[:, 4:6], AX, ALU.add))
                own.now(nc.vector.reciprocal(mix_w[:, 1:2], mix_w[:, 1:2]))
                own.now(nc.vector.tensor_scalar(mix_w[:, 6:8], mix_w[:, 4:6], mix_w[:, 1:2], AD ** -0.5, ALU.mult, ALU.mult))
                own.now(nc.vector.memset(powers[:], 1.0))
                own.now(nc.vector.memset(table[:], 1.0))
                for n in range(2):
                    own.now(nc.vector.tensor_tensor_scan(powers[:, n, 1:S], dp[:, n:n + 1].broadcast_to([AH, S - 1]),
                                                         table[:, 1:S], 1.0, ALU.mult, ALU.mult))
                own.now(nc.vector.tensor_scalar(powers[:, 0], powers[:, 0], mix_w[:, 6:7], None, ALU.mult))
                nc.vector.scalar_tensor_tensor(table[:], powers[:, 1], mix_w[:, 7:8], powers[:, 0], ALU.mult,
                                               ALU.add).then_inc(table_ok, 1)
                dve.wait_ge(table_ok, 1)
                tb = table[:]
                nc.vector.tensor_copy(table_r[:], bass.AP(tensor=tb.tensor, offset=tb.offset + S - 1,
                                                          ap=[list(tb.ap[0]), [-1, S]])).then_inc(table_ok, 1)
                dve.wait_ge(consts, 3)
                dve.sem_inc(y_ok, 1)
                dve.sem_inc(pk_ok, 4)
                own.now(nc.vector.memset(rt.masked_out[:], 3e38))
                first = own.n
                with dve.Fori(0, NB) as b:
                    own.base, own.n = b * DVE_A + first, 0

                    dve.wait_ge(x_first, 16)
                    normed(nc, dve, own, stats_ok, nm1, lambda t: x1[:, bass.ds(b * NT + t, 1)].rearrange("p a d -> p (a d)"),
                           xn, var1, rs1, b + 1)
                    dve.sem_inc(xn_ok, 1)
                    normed(nc, dve, own, stats_ok, nm2, lambda t: xn[:, t], xh, var2, rs2, b + 1)
                    dve.sem_inc(xh_ok, 1)
                    dve.wait_ge(x_rest, 16)
                    dve.wait_ge(rt_ps, b + 1)
                    i = choose_two(nc, dve, own, stats_ok, rt, banks[6][:, 0:NT * E].rearrange("p (t e) -> p t e", e=E), router_b,
                                   rt_done, rt_sh, rt_ex, b + 1, cw_all[:, bass.ds(b * NT, NT)])
                    dve.wait_ge(bcd_ok, b * NT + NT)
                    w = lambda j: dt_w[:, j]
                    own.now(nc.vector.tensor_tensor(w(0), bcd[:, :, 2 * NS:], head_rows[:, 1].unsqueeze(1).broadcast_to([P, NT, NH]), ALU.add))
                    nc.vector.tensor_scalar(w(0), w(0), 0.0, None, ALU.min).then_inc(dt_v, 1)
                    dve.wait_ge(dt_e, b + 1)
                    nc.vector.tensor_scalar(w(2), w(1), 1.0, None, ALU.add).then_inc(dt_u, 1)
                    dve.wait_ge(dt_u, b + 1)
                    own.now(nc.vector.tensor_scalar(w(4), w(2), -1.0, 1e-30, ALU.add, ALU.max))
                    own.now(nc.vector.reciprocal(w(5), w(4)))
                    own.now(nc.vector.tensor_tensor(w(6), w(1), w(5), ALU.mult))
                    dve.wait_ge(dt_l, b + 1)
                    own.now(nc.vector.tensor_tensor(w(7), w(3), w(6), ALU.mult))
                    own.now(nc.vector.tensor_scalar(w(7), w(7), 0.001, 0.1, ALU.max, ALU.min))
                    nc.vector.tensor_tensor(w(8), w(7), neg_a[:].unsqueeze(1).broadcast_to([P, NT, NH]), ALU.mult).then_inc(dt_w_ok, 1)
                    dve.wait_ge(dt_w_ok, b + 1)
                    nc.vector.tensor_scalar(la[:], w(8), LOG_MAX_DECAY, None, ALU.min).then_inc(la_ok, 1)
                    dve.wait_ge(dt_x, b + 1)
                    nc.vector.tensor_scalar(decay[:], w(9), 0.99, None, ALU.min).then_inc(decay_ok, 1)
                    dve.wait_ge(cum_ps, b + 1)
                    dve.wait_ge(ect_ok, b + 1)
                    cum = banks[4][:, 0:NT * NH].rearrange("p (t h) -> p t h", t=NT)
                    tot = banks[4][:, NT * NH:2 * NT * NH].rearrange("p (t h) -> p t h", t=NT)
                    own.now(nc.vector.tensor_scalar(ncum[:], cum, -1.0, None, ALU.mult))
                    nc.vector.tensor_tensor(tail[:], tot, ncum[:], ALU.add).then_inc(ncum_ok, 1)
                    for half in range(2):
                        dve.wait_ge(dbc_ok, b * 2 + half + 1)
                        dve.wait_ge(em_ok, b * 7 + 6)
                        for j, sq in enumerate((xT2[:, half], bT2[:])):
                            nc.vector.tensor_tensor_scan(scan_out[:, 2 * half + j], dec_bc[:, half], sq, 0.0,
                                                         ALU.mult, ALU.add).then_inc(scan_ok, 1)
                    dve.wait_ge(g_ps, b + 1)
                    for c in range(NT):
                        dve.wait_ge(l_ok, b * NT + c + 1)
                        g = banks[5][:, c * P:(c + 1) * P].unsqueeze(1).broadcast_to([P, NH, P])
                        if c >= 2:
                            dve.wait_ge(y_ps, b * NT + c - 1)
                        nc.vector.scalar_tensor_tensor(mt[:, c % 2], lmat[:, c % 2], 0.5, g, ALU.mult, ALU.mult).then_inc(m_ok, 1)
                        if c < NT - 1:
                            dve.wait_ge(h_ps, b * (NT - 1) + c + 1)
                            if c:
                                dve.wait_ge(y_ps, b * NT + c + 1)
                            for h in range(NH):
                                rows = slice(NS * (h // 2), NS * (h // 2 + 1))
                                st, up = state[rows, h * HD:(h + 1) * HD], banks[4][rows, h * HD:(h + 1) * HD]
                                if c == 0:
                                    i = own.did(nc.vector.tensor_copy(st, up))
                                else:
                                    i = own.did(nc.vector.scalar_tensor_tensor(st, st, e_ct[rows, 1, c, h:h + 1], up, ALU.mult, ALU.add))
                            own.after(i)
                            dve.sem_inc(h_ok, 1)
                        dve.wait_ge(y_ps, b * NT + c + 1)
                        dve.wait_ge(xd_ok, b * NT + c + 1)
                        yb = banks[6 + c % 2]
                        own.now(nc.vector.tensor_tensor(yt[:, 0], yb[:, 0:DI], xd[:, c].rearrange("p h d -> p (h d)"), ALU.add))
                        dst = y_all[:, bass.ds(b * NT + c, 1)].rearrange("p a d -> p (a d)")
                        if c:
                            own.now(nc.vector.tensor_tensor(yt[:, 1].rearrange("p (h d) -> p h d", h=NH),
                                                    yb[:, DI:].rearrange("p (h d) -> p h d", h=NH),
                                                    e_ct[:, 0, c].unsqueeze(2).broadcast_to([P, NH, HD]), ALU.mult))
                            nc.vector.tensor_tensor(dst, yt[:, 0], yt[:, 1], ALU.add).then_inc(y_ok, 1)
                        else:
                            nc.vector.tensor_copy(dst, yt[:, 0]).then_inc(y_ok, 1)
                    for k in range(4):
                        dve.wait_ge(scT_ps, b * 4 + k + 1)
                        nc.vector.tensor_reduce(pk[:, k], banks[2 + k % 2][:].rearrange("p (t n) -> p t n", n=HD), AX,
                                                ALU.max).then_inc(pk_ok, 1)
                        if k % 2:
                            dve.wait_ge(pk_ok, b * 4 + 4 + k + 1)
                            i = own.did(nc.vector.tensor_tensor(peak[:, bass.ds(b, 1), k // 2].rearrange("p a c -> p (a c)"),
                                                                pk[:, k - 1], pk[:, k], ALU.mult))
                    assert own.n == DVE_A, own.n



        with ExitStack() as work:
            wb = in_scope(work)
            STEPS = 32
            peak1 = wb("peak1", [P, 1])
            peak_all = wb("peak_all", [P, 1])
            safe = wb("safe", [P, 1], I32)
            x_steps = wb("x_steps", [P, 2, S])
            d_steps = wb("d_steps", [P, 2, S])
            y_steps = wb("y_steps", [P, 2, S])
            bc_steps = wb("bc_steps", [P, STEPS, 2 * NS])
            d_col = wb("d_col", [P, 2])
            h_st = wb("h_st", [P, 2, NS])
            h_in = wb("h_in", [P, 2, NS])
            names = ("peak1", "peak_all", "safe", "x_in", "bc_in", "bc_used", "own", "y_ok", "yT_ps", "y_used", "d_in", "gap")
            G = {n: sem("f_" + n) for n in names}
            block = work.enter_context(nc.Block())

            @block.gpsimd
            def _(pool):
                pool.wait_ge(G["peak1"], 1)
                nc.gpsimd.partition_all_reduce(peak_all[:], peak1[:], P, bass.bass_isa.ReduceOp.max).then_inc(G["peak_all"], 1)

            @block.sync
            def _(sp):
                for h in range(NH):
                    dst = d_col[HD * (h % 2):HD * (h % 2 + 1), h // 2:h // 2 + 1]
                    d_h = ins["Dparam"]
                    sp.dma_start(dst, bass.AP(tensor=d_h.tensor, offset=d_h.offset + h, ap=[[0, HD], [1, 1]])).then_inc(G["d_in"], 16)
                sp.wait_ge(G["d_in"], 16 * NH)
                sp.wait_ge(G["safe"], 1)
                all_safe = sp.value_load(safe[0:1, 0:1], min_val=0, max_val=1)
                with sp.If(all_safe == 0):
                    sp.sem_inc(G["bc_used"], 1)
                    with sp.Fori(0, NB) as b:
                        sp.wait_ge(G["y_used"], b + 1)
                        sp.dma_start(x_steps[:], xT_d[bass.ds(b, 1)].rearrange("a p h s -> p (a h) s")).then_inc(G["x_in"], 16)
                        sp.dma_start(d_steps[:], dec_d[bass.ds(b, 1)].rearrange("a p h s -> p (a h) s")).then_inc(G["x_in"], 16)
                        with sp.Fori(0, S // STEPS) as c:
                            sp.wait_ge(G["bc_used"], b * (S // STEPS) + c + 1)
                            src = bc_d.rearrange("b t p n -> (b t p) n")[bass.ds(b * S + c * STEPS, STEPS)]
                            sp.dma_start(bc_steps[:], src.partition_broadcast(P)).then_inc(G["bc_in"], 16)
                with sp.Else():
                    sp.nop()

            @block.tensor
            def _(pe):
                pe.wait_ge(G["safe"], 1)
                all_safe = pe.value_load(safe[0:1, 0:1], min_val=0, max_val=1)
                with pe.If(all_safe == 0):
                    with pe.Fori(0, NB) as b:
                        pe.wait_ge(G["y_ok"], b + 1)
                        for t in range(NT):
                            for half in range(2):
                                i = pe.transpose(banks[t][:, half * P:(half + 1) * P], y_steps[:, half, t * P:(t + 1) * P], ident[:])
                        i.then_inc(G["yT_ps"], 1)
                with pe.Else():
                    pe.nop()

            @block.vector
            def _(dve):
                nc.vector.tensor_reduce(peak1[:], peak[:].rearrange("p b a c -> p (b a c)"), AX, ALU.max).then_inc(G["peak1"], 1)
                dve.wait_ge(G["peak_all"], 1)
                nc.vector.tensor_scalar(safe[:], peak_all[:], SAFE, None, ALU.is_le).then_inc(G["safe"], 1)
                dve.wait_ge(G["safe"], 1)
                all_safe = dve.value_load(safe[0:1, 0:1], min_val=0, max_val=1)
                with dve.If(all_safe == 0):
                    own = Chain(dve, G["own"])
                    dve.sem_inc(G["y_used"], 1)
                    dve.wait_ge(G["d_in"], 16 * NH)
                    dve.sem_inc(G["gap"], 1)
                    PER_STEP, PER_SEQ = 6, 6 * S + 1 + 2 + NT
                    with dve.Fori(0, NB) as b:
                        own.base, own.n = b * PER_SEQ, 0
                        own.now(nc.vector.memset(h_st[:], 0.0))
                        dve.wait_ge(G["x_in"], b * 32 + 32)
                        dve.sem_inc(G["gap"], 1)
                        with dve.Fori(0, S // STEPS) as c:
                            dve.wait_ge(G["bc_in"], (b * (S // STEPS) + c + 1) * 16)
                            dve.sem_inc(G["gap"], 1)
                            with dve.Fori(0, STEPS) as s:
                                t = c * STEPS + s
                                own.base, own.n = b * PER_SEQ + 1 + t * PER_STEP, 0
                                at = lambda x: x[:, :, bass.ds(t, 1)].broadcast_to([P, 2, NS])
                                bc = lambda k: bc_steps[:, bass.ds(s, 1), k * NS:(k + 1) * NS].broadcast_to([P, 2, NS])
                                own.now(nc.vector.tensor_tensor(h_st[:], h_st[:], at(d_steps), ALU.mult))
                                own.now(nc.vector.tensor_tensor(h_in[:], bc(0), at(x_steps), ALU.mult))
                                own.now(nc.vector.tensor_tensor(h_st[:], h_st[:], h_in[:], ALU.add))
                                own.now(nc.vector.tensor_scalar(h_st[:], h_st[:], -CLIP, CLIP, ALU.max, ALU.min))
                                own.now(nc.vector.tensor_tensor(h_in[:], h_st[:], bc(1), ALU.mult))
                                own.now(nc.vector.tensor_reduce(y_steps[:, :, bass.ds(t, 1)], h_in[:], AX, ALU.add))
                            dve.sem_inc(G["bc_used"], 1)
                        own.base, own.n = b * PER_SEQ + 1 + S * PER_STEP, 0
                        for half in range(2):
                            i = own.did(nc.vector.scalar_tensor_tensor(y_steps[:, half], x_steps[:, half], d_col[:, half:half + 1],
                                                                       y_steps[:, half], ALU.mult, ALU.add))
                        own.after(i)
                        dve.sem_inc(G["y_ok"], 1)
                        dve.wait_ge(G["yT_ps"], b + 1)
                        for t in range(NT):
                            i = own.did(nc.vector.tensor_copy(y_all[:, bass.ds(b * NT + t, 1)].rearrange("p a d -> p (a d)"),
                                                              banks[t][:, 0:DI]))
                        own.after(i)
                        dve.sem_inc(G["y_used"], 1)
                with dve.Else():
                    dve.nop()

        with ExitStack() as work:
            wb = in_scope(work)
            sg = wb("sg", [P, 2, S])
            eo = wb("eo", [P, 2, 2, S])
            cw = wb("cw", [P, NT, E])
            (g_ps2, u_ps, sg_ok, eo_ok, o_ps, o_ok, zs_ok, gate_ok, own_b, own_ab) = (
                sem(n) for n in ("g_ps2", "u_ps", "sg_ok", "eo_ok", "o_ps", "o_ok", "zs_ok", "gate_ok", "own_b", "own_ab"))
            NK = 2 * (1 + E)
            block = work.enter_context(nc.Block())

            @block.tensor
            def _(pe):
                pe.wait_ge(wts_b, 16 * 8)
                pe.sem_inc(o_ps, 2)
                with pe.Fori(0, NB) as b:
                    xT_b = xnT[:, bass.ds(b, 1)].rearrange("p a s -> p (a s)")

                    def up(e):
                        for m in range(2):
                            k = 2 * e + m
                            pe.wait_ge(eo_ok, b * NK + k + 1)
                            pe.matmul(banks[2 * (k % 2)][:], w13[:, e, 0, m * P:(m + 1) * P], xT_b,
                                      start=True, stop=True).then_inc(g_ps2, 1)
                            pe.matmul(banks[2 * (k % 2) + 1][:], w13[:, e, 1, m * P:(m + 1) * P], xT_b,
                                      start=True, stop=True).then_inc(u_ps, 1)

                    def down(e):
                        pe.wait_ge(eo_ok, b * NK + 2 * (e + 1) + 2)
                        pe.wait_ge(o_ok, b * (1 + E) + e + 1)
                        for t in range(NT):
                            for m in range(2):
                                i = pe.matmul(banks[4 + e % 2][:, t * P:(t + 1) * P], eo[:, e % 2, m, t * P:(t + 1) * P],
                                              w2[:, e, m], start=(m == 0), stop=(m == 1))
                        i.then_inc(o_ps, 1)

                    up(0)
                    for e in range(1 + E):
                        if e < E:
                            up(e + 1)
                        down(e)

            @block.scalar
            def _(act):
                nc.scalar.preload_act_table(ACT.Silu)
                with act.Fori(0, NB) as b:
                    for k in range(NK):
                        act.wait_ge(g_ps2, b * NK + k + 1)
                        act.wait_ge(eo_ok, b * NK + k + 1)
                        nc.scalar.activation(sg[:, k % 2], banks[2 * (k % 2)][:], ACT.Silu).then_inc(sg_ok, 1)
                        if k % 4 == 3:
                            zt = z_all[:, bass.ds(b * NT + k // 4, 1)].rearrange("p a d -> p (a d)")
                            nc.scalar.activation(zt, zt, ACT.Silu).then_inc(zs_ok, 1)

            @block.vector
            def _(dve):
                own = Chain(dve, own_b)
                dve.sem_inc(eo_ok, 2)
                dve.sem_inc(o_ok, 2)
                with dve.Fori(0, NB) as b:
                    own.base, own.n = b * DVE_B, 0
                    own.now(nc.vector.tensor_copy(cw[:], cw_all[:, bass.ds(b * NT, NT)]))

                    def combine(e):
                        dve.wait_ge(o_ps, b * (1 + E) + e + 1 + 2)
                        bank = banks[4 + e % 2]
                        if e == 0:
                            xb = x1[:, bass.ds(b * NT, NT)].rearrange("p t d -> p (t d)")
                            k = own.did(nc.vector.tensor_tensor(xb, bank[:], xb, ALU.add))
                        else:
                            for t in range(NT):
                                xt = x1[:, bass.ds(b * NT + t, 1)].rearrange("p a d -> p (a d)")
                                k = own.did(nc.vector.scalar_tensor_tensor(xt, bank[:, t * P:(t + 1) * P],
                                                                           cw[:, t, e - 1:e], xt, ALU.mult, ALU.add))
                        own.after(k)
                        dve.sem_inc(o_ok, 1)

                    for k in range(NK):
                        e, m = k // 2, k % 2
                        dve.wait_ge(sg_ok, b * NK + k + 1)
                        dve.wait_ge(u_ps, b * NK + k + 1)
                        dve.wait_ge(o_ps, b * (1 + E) + e + 1)
                        nc.vector.tensor_tensor(eo[:, e % 2, m], sg[:, m], banks[2 * m + 1][:], ALU.mult).then_inc(eo_ok, 1)
                        if m and e:
                            combine(e - 1)
                        if k % 4 == 1 and k > 4:
                            t = k // 4 - 1
                            dve.wait_ge(zs_ok, b * NT + t + 1)
                            yt_ = y_all[:, bass.ds(b * NT + t, 1)].rearrange("p a d -> p (a d)")
                            zt = z_all[:, bass.ds(b * NT + t, 1)].rearrange("p a d -> p (a d)")
                            nc.vector.tensor_tensor(yt_, yt_, zt, ALU.mult).then_inc(gate_ok, 1)
                    combine(E)
                    assert own.n == DVE_B, own.n

        early.close()
        sb_late = in_scope(ctx)
        mask = sb_late("mask", [P, AH, MW])
        v3 = sb_late("v3", [P, TT, 3, DM], BF16)

        with ExitStack() as work:
            wb = in_scope(work)
            nmy, nmo, nmx = Norm(wb, "nmy"), Norm(wb, "nmo"), Norm(wb, "nmx")
            yn = wb("yn", [P, NT, DI])
            yT = wb("yT", [P, 2, S])
            oc = wb("oc", [P, NT, DM])
            on = wb("on", [P, NT, DM])
            x2n = wb("x2n", [P, NT, DM])
            x2T = wb("x2T", [P, S])
            qk = wb("qk", [P, 2, S])
            vt = wb("vt", [P, NT, DM])
            gw = wb("gw", [P, NT, E])
            gwT = wb("gwT", [E, S])
            onw = wb("onw", [P, NT, DM])
            onb = wb("onb", [P, NT, DM])
            parts = wb("parts", [P, 3, 2, S], BF16)
            rest = wb("rest", [P, 2, S])
            vrest = wb("vrest", [P, NT, DM])
            rt2 = Router(wb, "rt2")
            names = ("vy", "ry", "vo", "ro", "vx", "rx", "yn_ok", "yT_ps", "yT_ok", "out_ps", "out_ok", "x2_ok", "x2T_ps",
                     "x2T_ok", "lg_ps", "lg_ok", "sh_ok", "ex_ok", "qk_ps", "qk_ok", "split_ok", "kept", "v_ps", "v_ok",
                     "gw_ok", "gwT_ps", "gwT_ok", "bias_ps", "ex_ps", "mix_ok", "own_c", "own_ac", "own_g", "own_p", "on_ok", "aff_ok", "p2_ok", "v2_ok", "v3_ok")
            C = {n: sem("c_" + n) for n in names}
            block = work.enter_context(nc.Block())

            @block.sync
            def _(sp):
                sp.wait_ge(mirrored, 32)
                for h in range(AH):
                    src = bass.AP(tensor=mirror_d.tensor, offset=mirror_d.offset + h * 2 * S,
                                  ap=[[1, P], [1, MW]])
                    sp.dma_start(mask[:, h], src).then_inc(mask_in, 16)
                sp.sem_inc(C["kept"], 16)
                with sp.Fori(0, NB) as b:
                    sp.wait_ge(C["split_ok"], b + 2)
                    for j in range(2):
                        for i in range(3):
                            sp.dma_start(parts_d[j, i, bass.ds(b, 1)].rearrange("a p s -> p (a s)"),
                                         parts[:, i, j]).then_inc(C["kept"], 16)
                sp.wait_ge(C["kept"], 16 + 6 * 16 * NB)
                sp.wait_ge(mask_in, 16 * AH)

            @block.gpsimd
            def _(pool):
                pool.sem_inc(C["split_ok"], 1)
                pool.sem_inc(C["v3_ok"], 1)
                with pool.Fori(0, NB) as b:
                    pool.wait_ge(C["on_ok"], b + 1)
                    rows = lambda j: no_rows[:, j].unsqueeze(1).broadcast_to([P, NT, DM])
                    nc.gpsimd.tensor_tensor(onw[:], on[:], rows(0), ALU.mult).then_inc(C["own_p"], 1)
                    pool.wait_ge(C["own_p"], b + 1)
                    nc.gpsimd.tensor_tensor(onb[:], onw[:], rows(1), ALU.add).then_inc(C["aff_ok"], 1)
                    pool.wait_ge(C["p2_ok"], b + 1)
                    nc.gpsimd.tensor_tensor(parts[:, 2], rest[:], parts[:, 1], ALU.subtract).then_inc(C["split_ok"], 1)
                    pool.wait_ge(C["v2_ok"], b + 1)
                    nc.gpsimd.tensor_tensor(v3[:, bass.ds(b * NT, NT), 2], vrest[:], v3[:, bass.ds(b * NT, NT), 1],
                                            ALU.subtract).then_inc(C["v3_ok"], 1)

            @block.tensor
            def _(pe):
                pe.wait_ge(wts_c, 16 * WTS_C)
                with pe.Fori(0, NB) as b:
                    pe.wait_ge(C["yn_ok"], b + 1)
                    for half in range(2):
                        for t in range(NT):
                            i = pe.transpose(banks[half][:, t * P:(t + 1) * P], yn[:, t, half * P:(half + 1) * P], ident[:])
                        i.then_inc(C["yT_ps"], 1)
                    pe.wait_ge(C["yT_ok"], b * 2 + 2)
                    for t in range(NT):
                        for half in range(2):
                            i = pe.matmul(banks[2][:, t * P:(t + 1) * P], yT[:, half, t * P:(t + 1) * P], wo[:, half],
                                          start=(half == 0), stop=(half == 1))
                    i.then_inc(C["out_ps"], 1)
                    pe.wait_ge(C["x2_ok"], b + 1)
                    for t in range(NT):
                        i = pe.transpose(banks[3][:, t * P:(t + 1) * P], x2n[:, t], ident[:])
                    i.then_inc(C["x2T_ps"], 1)
                    pe.wait_ge(C["x2T_ok"], b + 1)
                    for t in range(NT):
                        i = pe.matmul(banks[6][:, t * E:(t + 1) * E], x2T[:, t * P:(t + 1) * P], gate_w[:], start=True, stop=True)
                    i.then_inc(C["lg_ps"], 1)
                    for j in range(2):
                        pe.matmul(banks[4 + j][:], wqkv[:, j], x2T[:], start=True, stop=True).then_inc(C["qk_ps"], 1)
                    for t in range(NT):
                        i = pe.matmul(banks[7][:, t * P:(t + 1) * P], x2T[:, t * P:(t + 1) * P], wqkv[:, 2], start=True, stop=True)
                    i.then_inc(C["v_ps"], 1)
                    def experts(t):
                        for j in range(2):
                            i = pe.matmul(banks[2 * (t % 2) + j][:], x2T[:, t * P:(t + 1) * P],
                                          ew[:, 4 * j:4 * j + 4].rearrange("p e o -> p (e o)"), start=True, stop=True)
                        i.then_inc(C["ex_ps"], 1)
                    experts(0)
                    experts(1)
                    pe.wait_ge(C["gw_ok"], b + 1)
                    for t in range(NT):
                        i = pe.transpose(banks[4][0:E, t * P:(t + 1) * P], gw[:, t], ident[:])
                    i.then_inc(C["gwT_ps"], 1)
                    pe.wait_ge(C["gwT_ok"], b + 1)
                    for t in range(NT):
                        i = pe.matmul(banks[5][:, t * P:(t + 1) * P], gwT[:, t * P:(t + 1) * P], eb[:], start=True, stop=True)
                    i.then_inc(C["bias_ps"], 1)
                    pe.wait_ge(C["mix_ok"], b * 3 + 2)
                    experts(2)
                    experts(3)

            @block.scalar
            def _(act):
                own = Chain(act, C["own_ac"])
                nc.scalar.preload_act_table_set("natural_log_exp_and_others")
                act.wait_ge(wts_c, 16 * WTS_C)
                with act.Fori(0, NB) as b:
                    own.base, own.n = b * 3, 0
                    rsqrt_by_exp(nc, act, own, nmy, C["vy"], C["ry"], b + 1)
                    for half in range(2):
                        act.wait_ge(C["yT_ps"], b * 2 + half + 1)
                        nc.scalar.activation(yT[:, half], banks[half][:], ACT.Identity, scale=ln_cols[:, 0, half:half + 1],
                                             bias=ln_cols[:, 1, half:half + 1]).then_inc(C["yT_ok"], 1)
                    rsqrt_by_exp(nc, act, own, nmo, C["vo"], C["ro"], b + 1)
                    rsqrt_by_exp(nc, act, own, nmx, C["vx"], C["rx"], b + 1)
                    act.wait_ge(C["x2T_ps"], b + 1)
                    nc.scalar.copy(x2T[:], banks[3][:]).then_inc(C["x2T_ok"], 1)
                    for j in range(2):
                        act.wait_ge(C["qk_ps"], b * 2 + j + 1)
                        nc.scalar.activation(qk[:, j], banks[4 + j][:], ACT.Identity, bias=bqk[:, j:j + 1]).then_inc(C["qk_ok"], 1)
                    act.wait_ge(C["sh_ok"], b + 1)
                    nc.scalar.activation(rt2.ex[:], rt2.sh[:], ACT.Exp).then_inc(C["ex_ok"], 1)
                    act.wait_ge(C["gwT_ps"], b + 1)
                    nc.scalar.copy(gwT[:], banks[4][0:E, :]).then_inc(C["gwT_ok"], 1)
                    assert own.n == 3

            @block.vector
            def _(dve):
                own = Chain(dve, C["own_c"])
                dve.wait_ge(wts_c, 16 * WTS_C)
                own.now(nc.vector.memset(rt2.masked_out[:], 3e38))
                with dve.Fori(0, NB) as b:
                    own.base, own.n = b * DVE_C + 1, 0
                    tile_of = lambda x, t: x[:, bass.ds(b * NT + t, 1)].rearrange("p a d -> p (a d)")
                    tiles_of = lambda x: x[:, bass.ds(b * NT, NT)]
                    normed(nc, dve, own, C["own_g"], nmy, lambda t: tile_of(y_all, t), yn, C["vy"], C["ry"], b + 1)
                    dve.sem_inc(C["yn_ok"], 1)
                    dve.wait_ge(C["out_ps"], b + 1)
                    own.now(nc.vector.tensor_scalar(oc[:].rearrange("p t d -> p (t d)"), banks[2][:], -CLIP, CLIP, ALU.max, ALU.min))
                    normed(nc, dve, own, C["own_g"], nmo, lambda t: oc[:, t], on, C["vo"], C["ro"], b + 1)
                    dve.sem_inc(C["on_ok"], 1)
                    dve.wait_ge(C["aff_ok"], b + 1)
                    own.now(nc.vector.tensor_tensor(tiles_of(x1), tiles_of(x1), onb[:], ALU.add))
                    normed(nc, dve, own, C["own_g"], nmx, lambda t: tile_of(x1, t), x2n, C["vx"], C["rx"], b + 1)
                    dve.sem_inc(C["x2_ok"], 1)
                    dve.wait_ge(C["lg_ps"], b + 1)
                    i = choose_two(nc, dve, own, C["own_g"], rt2, banks[6][:, 0:NT * E].rearrange("p (t e) -> p t e", e=E),
                                   gate_b, C["lg_ok"], C["sh_ok"], C["ex_ok"], b + 1, gw[:])
                    own.after(i)
                    dve.sem_inc(C["gw_ok"], 1)
                    dve.wait_ge(C["qk_ok"], b * 2 + 2)
                    dve.wait_ge(C["kept"], b * 96 + 16)
                    own.now(nc.vector.tensor_copy(parts[:, 0], qk[:]))
                    dve.wait_ge(C["split_ok"], b + 1)
                    own.now(nc.vector.tensor_tensor(rest[:], qk[:], parts[:, 0], ALU.subtract))
                    nc.vector.tensor_copy(parts[:, 1], rest[:]).then_inc(C["p2_ok"], 1)
                    dve.wait_ge(C["v_ps"], b + 1)
                    own.now(nc.vector.tensor_tensor(vt[:], banks[7][:].rearrange("p (t d) -> p t d", t=NT),
                                                    bv_row[:].unsqueeze(1).broadcast_to([P, NT, DM]), ALU.add))
                    v_b = tiles_of(v3)
                    own.now(nc.vector.tensor_copy(v_b[:, :, 0], vt[:]))
                    dve.wait_ge(C["v3_ok"], b + 1)
                    own.now(nc.vector.tensor_tensor(vrest[:], vt[:], v_b[:, :, 0], ALU.subtract))
                    nc.vector.tensor_copy(v_b[:, :, 1], vrest[:]).then_inc(C["v2_ok"], 1)
                    dve.wait_ge(C["bias_ps"], b + 1)
                    own.now(nc.vector.tensor_tensor(tiles_of(x1), banks[5][:].rearrange("p (t d) -> p t d", t=NT), tiles_of(x1), ALU.add))
                    for pair in range(2):
                        dve.wait_ge(C["ex_ps"], b * NT + 2 * pair + 2)
                        for e in range(E):
                            for j in range(2):
                                t = 2 * pair + j
                                if e:
                                    own.after(own.n - 1)
                                xt = tile_of(x1, t)
                                i = own.did(nc.vector.scalar_tensor_tensor(
                                    xt, banks[2 * j + e // 4][:, (e % 4) * P:(e % 4 + 1) * P], gw[:, t, e:e + 1], xt, ALU.mult, ALU.add))
                        own.after(i)
                        dve.sem_inc(C["mix_ok"], 2 if pair == 0 else 1)
                    assert own.n == DVE_C, own.n

        att = sb_late("att", [P, TT, DM])
        with ExitStack() as work:
            wb = in_scope(work)
            NP = 9 * AD
            qx = wb("qx", [NP, 2, S], BF16)
            kx = wb("kx", [NP, 2, S], BF16)
            m_cur = wb("m_cur", [P, MW])
            sm = wb("sm", [P, 4, S])
            pr = wb("pr", [P, 4, S])
            hi = wb("hi", [P, 4, S], F16)
            lo = wb("lo", [P, 4, S], F16)
            mx = wb("mx", [P, 4])
            nmx = wb("nmx", [P, 4])
            rsum = wb("rsum", [P, 8])
            inv = wb("inv", [P, 2, NT])
            osum = wb("osum", [P, 2, NT, AD])
            names = ("s_ps", "mx_ok", "sm_ok", "pr_ok", "t_ps", "hi_ok", "lo_ok", "o_ps", "osum_ok", "o_ok", "inv_ok", "mask_ok", "gap", "gap_p")
            D = {n: sem("d_" + n) for n in names}
            qk_in = [sem("qk_in0"), sem("qk_in1")]
            UN = 8
            TURNS = AH * NB // 2
            block = work.enter_context(nc.Block())

            def wait(eng, s, base, k):
                if not isinstance(base, int) or base + k > 0:
                    eng.wait_ge(s, base + k)

            def turns(eng, turn):
                turn(0, (0, 0), None)
                with eng.Fori(1, NB // 2) as g:
                    turn(g, (0, g), (0, g - 1))
                with eng.Fori(1, AH) as h:
                    turn(h * (NB // 2), (h, 0), (h - 1, NB // 2 - 1))
                    with eng.Fori(1, NB // 2) as g:
                        turn(h * (NB // 2) + g, (h, g), (h, g - 1))
                turn(TURNS, None, (AH - 1, NB // 2 - 1))

            @block.sync
            def _(sp):
                def turn(it, here, before):
                    if here is None:
                        return
                    h, g = here
                    for j in range(2):
                        wait(sp, D["s_ps"], it * UN, -UN + 4 * j + 4)
                        for i in range(3):
                            for dst, part, rows in ((qx, 0, slice(i, i + 1)), (kx, 1, slice(0, 3))):
                                src = parts_d[part, rows, bass.ds(g * 2 + j, 1), bass.ds(h * AD, AD)]
                                src = src.rearrange("i a d s -> i (a d) s")
                                if part == 0:
                                    src = src.broadcast_to([3, AD, S])
                                sp.dma_start(dst[3 * AD * i:3 * AD * (i + 1), j], src).then_inc(qk_in[j], 16)
                turns(sp, turn)

            @block.tensor
            def _(pe):
                def turn(it, here, before):
                    n = it * UN
                    for u in range(UN):
                        if here is not None:
                            j, qt = u // 4, u % 4
                            if qt == 0:
                                pe.wait_ge(qk_in[j], it * 96 + 96)
                            wait(pe, D["mx_ok"], n, u - 1)
                            pe.matmul(banks[u % 2][:], qx[:, j, qt * P:(qt + 1) * P], kx[:, j], start=True,
                                      stop=True).then_inc(D["s_ps"], 1)
                        if before is not None or u >= 2:
                            if here is not None or u < 2:
                                v = (u - 2) % 4
                                pe.wait_ge(D["pr_ok"], n + u - 1)
                                wait(pe, D["lo_ok"], n, u - 5)
                                for kt in range(NT):
                                    i = pe.transpose(banks[2 + v][:, kt * P:(kt + 1) * P], pr[:, v, kt * P:(kt + 1) * P], ident[:])
                                i.then_inc(D["t_ps"], 1)
                        if (before is not None or u >= 5) and (here is not None or u < 5):
                            v = (u - 5) % 4
                            h, g = here if u >= 5 else before
                            j = 1 if 1 <= u < 5 else 0
                            pe.wait_ge(D["lo_ok"], n + u - 4)
                            pe.wait_ge(D["hi_ok"], n + u - 4)
                            if v == 0:
                                pe.wait_ge(D["osum_ok"], it * 2 + (1 if u >= 5 else 0))
                            for kt in range(NT):
                                vv = v3[:, bass.ds((g * 2 + j) * NT + kt, 1), :, bass.ds(h * AD, AD)].rearrange("p a c d -> p (a c) d")
                                for part in (hi, lo):
                                    i = pe.matmul(banks[6 + j][:, v * 3 * AD:(v + 1) * 3 * AD], part[:, v, kt * P:(kt + 1) * P], vv,
                                                  start=(kt == 0 and part is hi and v == 0), stop=True, skip_group_check=True)
                            i.then_inc(D["o_ps"], 1)
                turns(pe, turn)

            @block.scalar
            def _(act):
                nc.scalar.preload_act_table(ACT.Exp)

                def turn(it, here, before):
                    n = it * UN
                    for u in range(UN):
                        if here is not None:
                            v = u % 4
                            act.wait_ge(D["sm_ok"], n + u + 1)
                            wait(act, D["t_ps"], n, u - 3)
                            nc.scalar.activation(pr[:, v], sm[:, v], ACT.Exp, bias=nmx[:, v:v + 1],
                                                 accum_out=rsum[:, u:u + 1]).then_inc(D["pr_ok"], 1)
                        if (before is not None or u >= 2) and (here is not None or u < 2):
                            v = (u - 2) % 4
                            act.wait_ge(D["t_ps"], n + u - 1)
                            wait(act, D["o_ps"], n, u - 5)
                            nc.scalar.copy(hi[:, v], banks[2 + v][:]).then_inc(D["hi_ok"], 1)
                turns(act, turn)

            @block.vector
            def _(dve):
                def outputs(k, j):
                    dve.wait_ge(D["o_ps"], 4 * k)
                    dve.wait_ge(D["o_ok"], k)
                    o = banks[6 + j][:, 0:NT * 3 * AD].rearrange("p (t c d) -> p t d c", t=NT, c=3)
                    nc.vector.tensor_reduce(osum[:, j], o, AX, ALU.add).then_inc(D["osum_ok"], 1)

                def turn(it, here, before):
                    n = it * UN
                    if here is not None and (isinstance(here[1], int) and here[1] == 0):
                        wait(dve, D["mx_ok"], n, 0)
                        mb = m_cur[:]
                        nc.vector.tensor_copy(bass.AP(tensor=mb.tensor, offset=mb.offset + MW - 1, ap=[list(mb.ap[0]), [-1, MW]]),
                                              mask[:, bass.ds(here[0], 1)].rearrange("p a c -> p (a c)")).then_inc(D["mask_ok"], 1)
                        dve.wait_ge(D["mask_ok"], here[0] + 1)
                    for u in range(UN):
                        if here is not None:
                            v, qt = u % 4, u % 4
                            dve.wait_ge(D["s_ps"], n + u + 1)
                            wait(dve, D["pr_ok"], n, u - 3)
                            dve.sem_inc(D["gap"], 1)
                            first = (NT - 1 - qt) * P
                            nc.vector.tensor_tensor_reduce(sm[:, v], banks[u % 2][:], m_cur[:, first:first + S], 1.0, -3e38,
                                                           ALU.mult, ALU.max, mx[:, v:v + 1]).then_inc(D["mx_ok"], 1)
                        if (before is not None or u >= 4) and (here is not None or u < 4):
                            w = (u - 4) % 4
                            dve.wait_ge(D["hi_ok"], n + u - 3)
                            wait(dve, D["o_ps"], n, u - 7)
                            nc.vector.tensor_tensor(lo[:, w], banks[2 + w][:], hi[:, w], ALU.subtract).then_inc(D["lo_ok"], 1)
                        if u == 1 and before is not None:
                            outputs(it * 2 - 1, 0)
                        if u == 2 and before is not None:
                            dve.wait_ge(D["pr_ok"], n)
                            dve.wait_ge(D["o_ok"], it * 2)
                            nc.vector.reciprocal(inv[:, 1], rsum[:, 4:8]).then_inc(D["inv_ok"], 1)
                        if u == 5 and before is not None:
                            outputs(it * 2, 1)
                        if u == 6 and here is not None:
                            dve.wait_ge(D["pr_ok"], n + 4)
                            dve.wait_ge(D["o_ok"], it * 2 + 1)
                            nc.vector.reciprocal(inv[:, 0], rsum[:, 0:4]).then_inc(D["inv_ok"], 1)
                dve.sem_inc(D["osum_ok"], 2)
                turns(dve, turn)

            @block.gpsimd
            def _(pool):
                def divided(k, h, g, j):
                    pool.wait_ge(D["osum_ok"], k + 2)
                    pool.wait_ge(D["inv_ok"], k)
                    nc.gpsimd.tensor_tensor(att[:, bass.ds((g * 2 + j) * NT, NT), bass.ds(h * AD, AD)], osum[:, j],
                                            inv[:, j].unsqueeze(2).broadcast_to([P, NT, AD]), ALU.mult).then_inc(D["o_ok"], 1)

                def turn(it, here, before):
                    n = it * UN
                    for u in range(UN):
                        if here is not None:
                            v = u % 4
                            pool.wait_ge(D["mx_ok"], n + u + 1)
                            wait(pool, D["pr_ok"], n, u - 3)
                            pool.sem_inc(D["gap_p"], 1)
                            nc.gpsimd.tensor_scalar(nmx[:, v:v + 1], mx[:, v:v + 1], -1.0, None, ALU.mult).then_inc(D["sm_ok"], 1)
                        if u == 2 and before is not None:
                            divided(it * 2 - 1, *before, 0)
                        if u == 6 and before is not None:
                            divided(it * 2, *before, 1)
                pool.sem_inc(D["o_ok"], 2)
                turns(pool, turn)

        with ExitStack() as work:
            wb = in_scope(work)
            aT = wb("aT", [P, 2, S])
            names = ("aT_ps", "aT_ok", "y_ps", "x_ok", "done", "own_e")
            F = {n: sem("e_" + n) for n in names}
            out_v = out.rearrange("b (t p) d -> p b t d", p=P)
            block = work.enter_context(nc.Block())

            @block.tensor
            def _(pe):
                for b in range(NB):
                    if b >= 2:
                        pe.wait_ge(F["aT_ok"], b - 1)
                    for t in range(NT):
                        i = pe.transpose(banks[b % 2][:, t * P:(t + 1) * P], att[:, b * NT + t], ident[:])
                    i.then_inc(F["aT_ps"], 1)
                    pe.wait_ge(F["aT_ok"], b + 1)
                    if b >= 2:
                        pe.wait_ge(F["x_ok"], b - 1)
                    for t in range(NT):
                        i = pe.matmul(banks[2 + b % 2][:, t * P:(t + 1) * P], aT[:, b % 2, t * P:(t + 1) * P], w_att[:], start=True, stop=True)
                    i.then_inc(F["y_ps"], 1)

            @block.scalar
            def _(act):
                for b in range(NB):
                    act.wait_ge(F["aT_ps"], b + 1)
                    if b >= 2:
                        act.wait_ge(F["y_ps"], b - 1)
                    nc.scalar.copy(aT[:, b % 2], banks[b % 2][:]).then_inc(F["aT_ok"], 1)

            @block.vector
            def _(dve):
                own = Chain(dve, F["own_e"])
                own.now(nc.vector.tensor_tensor(x1[:], x1[:], bo_row[:].unsqueeze(1).broadcast_to([P, TT, DM]), ALU.add))
                for b in range(NB):
                    dve.wait_ge(F["y_ps"], b + 1)
                    xb = x1[:, b * NT:(b + 1) * NT].rearrange("p t d -> p (t d)")
                    nc.vector.tensor_tensor(xb, banks[2 + b % 2][:], xb, ALU.add).then_inc(F["x_ok"], 1)

            @block.sync
            def _(sp):
                for b in range(NB):
                    sp.wait_ge(F["x_ok"], b + 1)
                    sp.dma_start(out_v[:, b], x1[:, b * NT:(b + 1) * NT]).then_inc(F["done"], 16)
                sp.wait_ge(F["done"], 16 * NB)


def layout(inputs):
    import numpy as np
    a = {k: np.asarray(v) for k, v in inputs.items()}
    t = lambda n: np.ascontiguousarray(a[n].T)
    lay = {"x": a["L0_attn_x"], "in_wT": t("L0_attn_in_proj_w"), "out_wT": t("L0_attn_out_proj_w"),
           "router_wT": t("L0_ffn_router_w"), "experts_bias": a["L0_ffn_experts_bias"],
           "wqT": np.ascontiguousarray(a["L1_attn_Wq"].T), "wkT": np.ascontiguousarray(a["L1_attn_Wk"].T),
           "wvT": np.ascontiguousarray(a["L1_attn_Wv"].T), "woT": np.ascontiguousarray(a["L1_attn_Wo"].T),
           "gate_wT": t("L1_ffn_gate_w"), "gate_b": a["L1_ffn_gate_b"],
           "expert_w": a["L1_ffn_expert_w"], "expert_b": a["L1_ffn_expert_b"],
           "ident": np.eye(P, dtype=np.float32)}
    for n in ("bq", "bk", "bv", "bo", "decay_params", "mix_weights"):
        lay[n] = a["L1_attn_" + n]
    for n in ("w1", "w3", "w2", "sw1", "sw3", "sw2"):
        lay[n] = a["L0_ffn_" + n]
    for n in ("A_log", "dt_bias", "Dparam", "ln_w", "ln_b", "ni_w", "ni_b", "no_w", "no_b"):
        lay[n] = a["L0_attn_" + n]
    for n in ("ln_w", "ln_b", "bq", "bk"):
        lay[n] = np.ascontiguousarray(lay[n].reshape(-1, P).T)
    return lay


def kernel(**inputs):
    import numpy as np
    import concourse.bacc as bacc
    from concourse.bass_utils import run_bass_kernel_spmd

    nc = bacc.Bacc("TRN2", target_bir_lowering=False, num_devices=1)
    arrays = layout(inputs)
    ins = {n: nc.dram_tensor(f"in_{n}", a.shape, mybir.dt.from_np(a.dtype), kind="ExternalInput").ap()
           for n, a in arrays.items()}
    out = nc.dram_tensor("out", (NB, S, DM), F32, kind="ExternalOutput").ap()
    two_layers_kernel(nc, ins, out)
    result = run_bass_kernel_spmd(nc, [{f"in_{n}": a for n, a in arrays.items()}], core_ids=[0])
    return result.results[0]["out"]
```

```python
import math
from contextlib import ExitStack

import concourse.bass as bass
from concourse import mybir

F32 = mybir.dt.float32
F16 = mybir.dt.float16
BF16 = mybir.dt.bfloat16
I32 = mybir.dt.int32
ALU = mybir.AluOpType
ACT = mybir.ActivationFunctionType
AX = mybir.AxisListType.X

P = 128
NB, S, DM = 8, 512, 128
NT = S // P
TT = NB * NT
NH, HD = 4, 64
DI = NH * HD
NS = 64
E, FH = 8, 256
AH, AD = 16, 8
EPS = 1e-5
LOG_MAX_DECAY = math.log(0.99)
CLIP = 10.0
SAFE = 0.99 * CLIP * CLIP
MASKED = -1e30


DVE_A1, DVE_A2 = 32, 41
DVE_B = 38
DVE_CY, DVE_C1, DVE_C2 = 5, 33, 46
WTS_C = 17
MW = 896


class Chain:

    def __init__(self, eng, sem):
        self.eng, self.sem, self.base, self.n = eng, sem, 0, 0

    def did(self, ins):
        ins.then_inc(self.sem, 1)
        self.n += 1
        return self.n

    def after(self, k):
        self.eng.wait_ge(self.sem, self.base + k)

    def now(self, ins):
        self.after(self.did(ins))


class Norm:

    def __init__(self, sb, name):
        t = lambda n, *shape: sb(f"{name}_{n}", [P, NT, *shape])
        self.stats, self.mv, self.var, self.ln, self.rs, self.t, self.rstd = (
            t("stats", 6), t("mv", 2), t("var"), t("ln"), t("rs"), t("t"), t("rstd"))


def rsqrt_by_exp(nc, act, own, nm, var_ok, rs_ok, turn):
    act.wait_ge(var_ok, turn)
    own.now(nc.scalar.activation(nm.ln[:], nm.var[:], ACT.Ln))
    nc.scalar.activation(nm.rs[:], nm.ln[:], ACT.Exp, scale=-0.5).then_inc(rs_ok, 1)


def norm_stats(nc, dve, own, gap, nm, src, var_ok):
    dve.sem_inc(gap, 1)
    for t in range(NT):
        i = own.did(nc.vector.bn_stats(nm.stats[:, t], src(t)))
    own.after(i)
    dve.sem_inc(gap, 1)
    for t in range(NT):
        i = own.did(nc.vector.bn_aggr(nm.mv[:, t], nm.stats[:, t]))
    own.after(i)
    nc.vector.tensor_scalar(nm.var[:], nm.mv[:, :, 1], EPS, None, ALU.add).then_inc(var_ok, 1)


def norm_apply(nc, dve, own, nm, src, dst, rs_ok, turn):
    dve.wait_ge(rs_ok, turn)
    own.now(nc.vector.tensor_tensor(nm.t[:], nm.rs[:], nm.var[:], ALU.mult))
    own.now(nc.vector.tensor_tensor(nm.t[:], nm.t[:], nm.rs[:], ALU.mult))
    own.now(nc.vector.tensor_scalar(nm.t[:], nm.t[:], -0.5, 1.5, ALU.mult, ALU.add))
    own.now(nc.vector.tensor_tensor(nm.rstd[:], nm.t[:], nm.rs[:], ALU.mult))
    for t in range(NT):
        i = own.did(nc.vector.tensor_scalar(dst[:, t], src(t), nm.mv[:, t, 0:1], nm.rstd[:, t:t + 1],
                                            ALU.subtract, ALU.mult))
    own.after(i)


class Router:

    def __init__(self, sb, name):
        t = lambda n, *shape: sb(f"{name}_{n}", [P, NT, *shape])
        self.lg, self.m8, self.masked_out, self.rep = t("lg", E), t("m8", 8), t("kill", 8), t("rep", E)
        self.sh, self.ex, self.sum, self.inv = t("sh", E), t("ex", E), t("sum"), t("inv")


def choose_two(nc, dve, own, gap, rt, logits, bias, read_ok, shifted_ok, turn):
    nc.vector.tensor_tensor(rt.lg[:], logits, bias[:].unsqueeze(1).broadcast_to([P, NT, E]), ALU.add).then_inc(read_ok, 1)
    dve.wait_ge(read_ok, turn)
    dve.sem_inc(gap, 1)
    for t in range(NT):
        i = own.did(nc.vector.max(rt.m8[:, t], rt.lg[:, t]))
    own.after(i)
    nc.vector.tensor_tensor(rt.sh[:], rt.lg[:], rt.m8[:, :, 0:1].broadcast_to([P, NT, E]), ALU.subtract).then_inc(shifted_ok, 1)
    own.now(nc.vector.tensor_copy(rt.masked_out[:, :, 0:2], rt.m8[:, :, 0:2]))
    dve.sem_inc(gap, 1)
    for t in range(NT):
        i = own.did(nc.vector.match_replace(rt.rep[:, t], rt.masked_out[:, t], rt.lg[:, t], MASKED))
    own.after(i)
    own.now(nc.vector.tensor_tensor(rt.rep[:], rt.rep[:], rt.lg[:], ALU.not_equal))


def weigh_two(nc, dve, own, rt, exp_ok, turn, weights):
    dve.wait_ge(exp_ok, turn)
    own.now(nc.vector.tensor_tensor(rt.ex[:], rt.ex[:], rt.rep[:], ALU.mult))
    own.now(nc.vector.tensor_reduce(rt.sum[:], rt.ex[:], AX, ALU.add))
    own.now(nc.vector.reciprocal(rt.inv[:], rt.sum[:]))
    return own.did(nc.vector.tensor_tensor(weights, rt.ex[:], rt.inv[:].unsqueeze(2).broadcast_to([P, NT, E]), ALU.mult))


def two_layers_kernel(nc, ins, out):
    ctx = ExitStack()
    with ctx:
        def sb(name, shape, dt=F32):
            return ctx.enter_context(nc.sbuf_tensor(name, shape, dt))

        def in_scope(stack):
            return lambda name, shape, dt=F32: stack.enter_context(nc.sbuf_tensor(name, shape, dt))

        def dram(name, shape, dt=F32):
            return nc.dram_tensor(name, shape, dt, kind="Internal").ap()

        def sem(name):
            return ctx.enter_context(nc.semaphore(name))

        def row_on_all(ap, n):
            return bass.AP(tensor=ap.tensor, offset=ap.offset, ap=[[0, P], [1, n]])

        x1 = sb("x1", [P, TT, DM])
        y_all = sb("y_all", [P, TT, DI])
        ident = sb("ident", [P, P])
        ident_b = sb("ident_b", [P, P], BF16)
        peak = sb("peak", [P, NB, 2, NT * 2])
        y_bn = sb("y_bn", [P, TT, 6])
        wo = sb("wo", [P, 2, DM])
        ln_cols = sb("ln_cols", [P, 2, 2])
        no_rows = sb("no_rows", [P, 2, DM])
        wqkv = sb("wqkv", [P, 3, DM])
        w_att = sb("w_att", [P, DM])
        bqk = sb("bqk", [P, 2])
        bv_row = sb("bv_row", [P, DM])
        bo_row = sb("bo_row", [P, DM])
        gate_w = sb("gate_w", [P, E])
        gate_b = sb("gate_b", [P, E])
        ew = sb("ew", [P, E, DM])
        eb = sb("eb", [E, DM])
        dp = sb("dp", [AH, 2])
        mix = sb("mix", [AH, 2])
        early = ctx.enter_context(ExitStack())
        sb_early = in_scope(early)
        xnT = sb_early("xnT", [P, NB, S])
        z_all = sb_early("z_all", [P, TT, DI])
        w13 = sb_early("w13", [P, 1 + E, 2, FH])
        w2 = sb_early("w2", [P, 1 + E, 2, DM])
        cw_all = sb_early("cw_all", [P, TT, E])
        router_w = sb_early("router_w", [P, E])
        router_b = sb_early("router_b", [P, E])
        w_zx = sb_early("w_zx", [P, 2 * DI])
        w_bcd = sb_early("w_bcd", [P, 2 * NS + NH])
        w_bb = sb_early("w_bb", [P, 2, NS])
        w_cc = sb_early("w_cc", [P, 2, NS])
        ni = sb_early("ni", [P, 2])
        head_rows = sb_early("head_rows", [P, 3, NH])
        neg_a = sb_early("neg_a", [P, NH])
        upper = sb_early("upper", [P, P])
        ones = sb_early("ones", [P, P])
        strict_b = sb_early("strict_b", [P, P], BF16)
        d_row = sb_early("d_row", [P, NH, HD])

        xT_d = dram("xT_d", (NB, P, 2, S))
        dec_d = dram("dec_d", (NB, P, 2, S))
        bc_d = dram("bc_d", (NB, NT, P, 2 * NS))
        mirror_d = dram("mirror_d", (AH, 2 * S))
        parts_d = dram("parts_d", (2, 3, NB, P, S), BF16)
        mirrored, wts_m, wts_c, mask_in, mix_ex = (sem(n) for n in ("mirrored", "wts_m", "wts_c", "mask_in", "mix_ex"))

        banks = [ctx.enter_context(nc.psum_tensor(f"bank{i}", [P, 512], F32)) for i in range(8)]

        x_first, x_rest, wts, wts_b = sem("x_first"), sem("x_rest"), sem("wts"), sem("wts_b")
        consts = sem("consts")
        dve_own, dve_own1, act_own, pool_own = sem("dve_own"), sem("dve_own1"), sem("act_own"), sem("pool_own")
        var1, var2, rs1, rs2 = sem("var1"), sem("var2"), sem("rs1"), sem("rs2")
        stats_ok, xn_ok, xh_ok = sem('stats_ok'), sem("xn_ok"), sem("xh_ok")
        xnT_ps, xhT_ps, xnT_ok, xhT_ok = sem("xnT_ps"), sem("xhT_ps"), sem("xnT_ok"), sem("xhT_ok")
        zx_ps, zx_ok, bcd_ps, bcd_ok = sem("zx_ps"), sem("zx_ok"), sem("bcd_ps"), sem("bcd_ok")
        em_ps, em_ok = sem("em_ps"), sem("em_ok")
        dt_v, dt_e, dt_u, dt_l, dt_w_ok, dt_x = (sem(n) for n in ("dt_v", "dt_e", "dt_u", "dt_l", "dt_w_ok", "dt_x"))
        la_ok, decay_ok, cum_ps, ect_ok, ncum_ok, etail_ok = (
            sem(n) for n in ("la_ok", "decay_ok", "cum_ps", "ect_ok", "ncum_ok", "etail_ok"))
        dbc_ps, dbc_ok = sem("dbc_ps"), sem("dbc_ok")
        g_ok, g_ps, l_ps, l_ok, m_ok, xw_ok, xd_ok = (sem(n) for n in ("g_ok", "g_ps", "l_ps", "l_ok", "m_ok", "xw_ok", "xd_ok"))
        y_ps, y_ok, h_ps, h_ok = sem("y_ps"), sem("y_ok"), sem("h_ps"), sem("h_ok")
        spilled = sem("spilled")
        rt_ps, rt_sh, rt_ex, rt_done = (sem(n) for n in ("rt_ps", "rt_sh", "rt_ex", "rt_done"))
        scan_ok, scT_ps, pk_ok, xnT_all = sem("scan_ok"), sem("scT_ps"), sem("pk_ok"), sem("xnT_all")

        x_v = ins["x"].rearrange("b (t p) d -> p b t d", p=P)

        with ExitStack() as work:
            wb = in_scope(work)
            nm1, nm2 = Norm(wb, "nm1"), Norm(wb, "nm2")
            mix_w = wb("mix_w", [AH, 8])
            table_ok = sem("table_ok")
            xn = wb("xn", [P, NT, DM])
            xh = wb("xh", [P, NT, DM])
            xhT = wb("xhT", [P, S])
            xs = wb("xs", [P, NT, DI])
            bcd = wb("bcd", [P, NT, 2 * NS + NH])
            xT = wb("xT", [P, 2, S])
            xT2 = wb("xT2", [P, 2, S])
            bT = wb("bT", [P, S])
            bT2 = wb("bT2", [P, S])
            cT = wb("cT", [P, S])
            dt_w = wb("dt_w", [P, 12, NT, NH])
            decay = wb("decay", [P, NT, NH])
            la = wb("la", [P, NT, NH])
            ncum = wb("ncum", [P, NT, NH])
            tail = wb("tail", [P, NT, NH])
            e_ct = wb("e_ct", [P, 2, NT, NH])
            e_tail = wb("e_tail", [P, NT, NH])
            gram = wb("gram", [P, S])
            lmat = wb("lmat", [P, 2, NH, P])
            mt = wb("mt", [P, 2, NH, P])
            xw = wb("xw", [P, NT, NH, HD])
            xd = wb("xd", [P, NT, NH, HD])
            powers = xw[0:AH].rearrange("p t h d -> p (t h d)").rearrange("p (n s) -> p n s", n=2)
            table = xd[0:AH, 0:2].rearrange("p t h d -> p (t h d)")
            table_r = xd[0:AH, 2:4].rearrange("p t h d -> p (t h d)")
            yt = wb("yt", [P, 2, DI])
            state = wb("state", [P, 2, DI])
            scan_out = wb("scan_out", [P, 4, S])
            dec_bc = wb("dec_bc", [P, 2, S])
            xnc = wb("xnc", [P, S])
            pk = wb("pk", [P, 4, NT * 2])
            rt = Router(wb, "rt")


            block = work.enter_context(nc.Block())

            @block.sync
            def _(sp):
                x1v = x1[:].rearrange("p (b t) d -> p b t d", b=NB)
                sp.dma_start(x1v[:, 0], x_v[:, 0]).then_inc(x_first, 16)
                sp.dma_start(dp[:], ins["decay_params"]).then_inc(wts_m, 16)
                sp.dma_start(mix[:], ins["mix_weights"]).then_inc(wts_m, 16)
                sp.dma_start(ident[:], ins["ident"]).then_inc(wts, 16)
                sp.dma_start(ni[:, 0:1], ins["ni_w"].rearrange("(p a) -> p a", a=1)).then_inc(wts, 16)
                sp.dma_start(ni[:, 1:2], ins["ni_b"].rearrange("(p a) -> p a", a=1)).then_inc(wts, 16)
                sp.dma_start(w_zx[:], ins["in_wT"][:, 0:2 * DI]).then_inc(wts, 16)
                sp.dma_start(w_bcd[:], ins["in_wT"][:, 2 * DI:]).then_inc(wts, 16)
                for j in range(2):
                    sp.dma_start(w_bb[:, j], ins["in_wT"][:, 2 * DI:2 * DI + NS]).then_inc(wts, 16)
                    sp.dma_start(w_cc[:, j], ins["in_wT"][:, 2 * DI + NS:2 * DI + 2 * NS]).then_inc(wts, 16)
                for j, n in enumerate(("A_log", "dt_bias", "Dparam")):
                    sp.dma_start(head_rows[:, j], row_on_all(ins[n], NH)).then_inc(wts, 16)
                sp.dma_start(router_w[:], ins["router_wT"]).then_inc(wts, 16)
                sp.dma_start(router_b[:], row_on_all(ins["experts_bias"], E)).then_inc(wts, 16)
                sp.dma_start(x1v[:, 1:], x_v[:, 1:]).then_inc(x_rest, 16)
                sp.wait_ge(table_ok, 2)
                sp.dma_start(mirror_d[:, S - 1:2 * S - 1], table[:]).then_inc(mirrored, 16)
                sp.dma_start(mirror_d[:, 0:S - 1], table_r[:, 0:S - 1]).then_inc(mirrored, 16)
                for m in range(2):
                    sp.dma_start(w13[:, 0, m], ins[("sw1", "sw3")[m]][0]).then_inc(wts_b, 16)
                    sp.dma_start(w13[:, 1:, m], ins[("w1", "w3")[m]].rearrange("e d h -> d e h")).then_inc(wts_b, 16)
                    sp.dma_start(w2[:, 0, m], ins["sw2"][0, m * P:(m + 1) * P]).then_inc(wts_b, 16)
                    sp.dma_start(w2[:, 1:, m], ins["w2"][:, m * P:(m + 1) * P].rearrange("e h d -> h e d")).then_inc(wts_b, 16)
                load = lambda dst, src: sp.dma_start(dst, src).then_inc(wts_c, 16)
                load(wo[:], ins["out_wT"].rearrange("(j p) d -> p j d", p=P))
                load(ln_cols[:, 0], ins["ln_w"])
                load(ln_cols[:, 1], ins["ln_b"])
                load(no_rows[:, 0], row_on_all(ins["no_w"], DM))
                load(no_rows[:, 1], row_on_all(ins["no_b"], DM))
                for j, n in enumerate("qkv"):
                    load(wqkv[:, j], ins[f"w{n}T"])
                load(w_att[:], ins["woT"])
                load(bqk[:, 0:1], ins["bq"])
                load(bqk[:, 1:2], ins["bk"])
                load(bv_row[:], row_on_all(ins["bv"], DM))
                load(bo_row[:], row_on_all(ins["bo"], DM))
                load(gate_w[:], ins["gate_wT"])
                load(gate_b[:], row_on_all(ins["gate_b"], E))
                load(ew[:], ins["expert_w"].rearrange("e d o -> d e o"))
                load(eb[:], ins["expert_b"])
                sp.sem_inc(spilled, 16)
                with sp.Fori(0, NB) as b:
                    sp.wait_ge(bcd_ok, b * 2 + 2)
                    sp.dma_start(bc_d[bass.ds(b, 1)].rearrange("a t p n -> p (a t) n"),
                                 bcd[:, :, 0:2 * NS]).then_inc(spilled, 16)
                    sp.wait_ge(em_ok, b * 7 + 2)
                    sp.dma_start(xT_d[bass.ds(b, 1)].rearrange("a p h s -> p (a h) s"), xT[:]).then_inc(spilled, 16)
                    sp.wait_ge(dbc_ok, b * 2 + 2)
                    sp.dma_start(dec_d[bass.ds(b, 1)].rearrange("a p h s -> p (a h) s"), dec_bc[:]).then_inc(spilled, 16)
                sp.wait_ge(spilled, 16 + 48 * NB)
                sp.wait_ge(mirrored, 32)

            def ahead(eng, first_half, both_halves):
                first_half(0)
                with eng.Fori(0, NB - 1) as b:
                    both_halves(b, b + 1)
                both_halves(NB - 1, None)

            @block.gpsimd
            def _(pool):
                own = Chain(pool, pool_own)
                own.now(nc.gpsimd.memset(ones[:], 1.0))
                own.now(nc.gpsimd.affine_select(out=upper[:], in_=ones[:], compare_op=ALU.is_ge, fill=0.0, base=0,
                                                pattern=[[1, P]], channel_multiplier=-1))
                nc.gpsimd.memset(state[:], 0.0).then_inc(consts, 1)
                own.now(nc.gpsimd.memset(strict_b[:], 0.0))
                nc.gpsimd.affine_select(out=strict_b[:], in_=strict_b[:], compare_op=ALU.is_ge, fill=MASKED, base=0,
                                        pattern=[[1, P]], channel_multiplier=-1).then_inc(consts, 1)
                pool.wait_ge(wts, 16 * 14)
                nc.gpsimd.tensor_copy(ident_b[:], ident[:]).then_inc(consts, 1)
                own.now(nc.gpsimd.tensor_copy(d_row[:], head_rows[:, 2].unsqueeze(2).broadcast_to([P, NH, HD])))

                def first_half(b):
                    pool.wait_ge(xnT_ok, b + 1)
                    nc.gpsimd.tensor_copy(xnT[:, bass.ds(b, 1)].rearrange("p a s -> p (a s)"), xnc[:]).then_inc(xnT_all, 1)

                def both_halves(b, nxt):
                    pool.wait_ge(mirrored, 32)
                    pool.wait_ge(zx_ok, b * 2 * NT + 2 * NT)
                    pool.wait_ge(y_ok, b * NT + 1)
                    for t in range(NT):
                        nc.gpsimd.tensor_tensor(xd[:, t], xs[:, t].rearrange("p (h d) -> p h d", h=NH), d_row[:],
                                                ALU.mult).then_inc(xd_ok, 1)
                    pool.wait_ge(etail_ok, b + 1)
                    for t in range(NT - 1):
                        nc.gpsimd.tensor_tensor(xw[:, t], xs[:, t].rearrange("p (h d) -> p h d", h=NH),
                                                e_tail[:, t].unsqueeze(2).broadcast_to([P, NH, HD]),
                                                ALU.mult).then_inc(xw_ok, 1)
                    if nxt is not None:
                        first_half(nxt)

                pool.sem_inc(xnT_all, 1)
                ahead(pool, first_half, both_halves)

            @block.tensor
            def _(pe):
                pe.wait_ge(wts, 16 * 14)
                pe.wait_ge(consts, 3)

                def first_half(b):
                    pe.wait_ge(xn_ok, b + 1)
                    for t in range(NT):
                        i = pe.transpose(banks[0][:, t * P:(t + 1) * P], xn[:, t], ident[:])
                    i.then_inc(xnT_ps, 1)
                    pe.wait_ge(xh_ok, b + 1)
                    for t in range(NT):
                        i = pe.transpose(banks[1][:, t * P:(t + 1) * P], xh[:, t], ident[:])
                    i.then_inc(xhT_ps, 1)

                def both_halves(b, nxt):
                    pe.wait_ge(xhT_ok, b + 1)
                    for t in range(NT):
                        i = pe.matmul(banks[4 + t // 2][:, (t % 2) * DI:(t % 2) * DI + 2 * NS + NH], xhT[:, t * P:(t + 1) * P],
                                      w_bcd[:], start=True, stop=True)
                        if t % 2:
                            i.then_inc(bcd_ps, 1)
                    pe.wait_ge(xnT_ok, b + 1)
                    for t in range(NT):
                        if t >= 2:
                            pe.wait_ge(pk_ok, b * 4 + 1 + t)
                        pe.matmul(banks[t][:], xhT[:, t * P:(t + 1) * P], w_zx[:], start=True, stop=True).then_inc(zx_ps, 1)
                    pe.wait_ge(bcd_ok, b * 2 + 2)
                    for t in range(NT):
                        i = pe.matmul(banks[5][:, t * E:(t + 1) * E], xnc[:, t * P:(t + 1) * P], router_w[:], start=True, stop=True)
                    i.then_inc(rt_ps, 1)
                    pe.wait_ge(y_ok, b * NT + 1)
                    for j, (w, k) in enumerate(((w_zx[:, DI:DI + P], 0), (w_zx[:, DI + P:], 1),
                                                (w_bb[:].rearrange("p a n -> p (a n)"), 6),
                                                (w_cc[:].rearrange("p a n -> p (a n)"), 7))):
                        if k < 2:
                            pe.wait_ge(zx_ok, b * 2 * NT + 2 * (k + 1))
                        pe.matmul(banks[k][:], w, xhT[:], start=True, stop=True).then_inc(em_ps, 1)
                    pe.wait_ge(la_ok, b + 1)
                    lav = la[:].rearrange("p t h -> p (t h)")
                    pe.matmul(banks[4][:, 0:NT * NH], upper[:], lav, start=True, stop=True)
                    pe.matmul(banks[4][:, NT * NH:2 * NT * NH], ones[:], lav, start=False, stop=True,
                              skip_group_check=True).then_inc(cum_ps, 1)
                    pe.wait_ge(zx_ok, b * 2 * NT + 2 * NT)
                    pe.wait_ge(decay_ok, b + 1)
                    for half in range(2):
                        for t in range(NT):
                            for j in range(2):
                                h = 2 * half + j
                                i = pe.matmul(banks[2 + half][HD * j:HD * (j + 1), t * P:(t + 1) * P],
                                              decay[:, t, h:h + 1].broadcast_to([P, HD]), ident[:],
                                              start=(t == 0), stop=True, skip_group_check=True)
                        i.then_inc(dbc_ps, 1)

                    def decays(c):
                        k = banks[c % 2]
                        if c >= 2:
                            pe.wait_ge(l_ok, b * NT + c - 1)
                        pe.matmul(k[:], ident_b[:], strict_b[:].unsqueeze(1).broadcast_to([P, NH, P]),
                                  start=True, stop=True, skip_group_check=True)
                        for h in range(NH):
                            i = pe.matmul(k[:, h * P:(h + 1) * P], la[:, c, h:h + 1].broadcast_to([P, P]), upper[:],
                                          start=False, stop=True, skip_group_check=True)
                        i.then_inc(l_ps, 1)

                    pe.wait_ge(em_ok, b * 7 + 7)
                    decays(0)
                    pe.wait_ge(rt_done, b + 1)
                    for t in range(NT):
                        i = pe.matmul(banks[5][:, t * P:(t + 1) * P], bT[:, t * P:(t + 1) * P], cT[:, t * P:(t + 1) * P],
                                      start=(t == 0), stop=True, skip_group_check=True)
                    i.then_inc(g_ps, 1)
                    decays(1)
                    pe.wait_ge(ncum_ok, b + 1)
                    pe.wait_ge(ect_ok, b + 1)
                    for c in range(NT):
                        yb, hb = banks[6 + c % 2], banks[4 + c % 2][:, 0:DI]
                        if c < NT - 1:
                            pe.wait_ge(xw_ok, b * (NT - 1) + c + 1)
                            if c == 1:
                                pe.wait_ge(g_ok, b + 1)
                            if c >= 2:
                                pe.wait_ge(h_ok, b * (NT - 1) + c - 1)
                            for j in range(2):
                                i = pe.matmul(hb[NS * j:NS * (j + 1)], bcd[:, c, 0:NS],
                                              xw[:, c].rearrange("p h d -> p (h d)"), start=True, stop=True)
                            i.then_inc(h_ps, 1)
                        if c + 2 < NT:
                            decays(c + 2)
                        if c == NT - 1 and nxt is not None:
                            pe.wait_ge(l_ok, b * NT + NT)
                            first_half(nxt)
                        pe.wait_ge(m_ok, b * NT + c + 1)
                        if c >= 2:
                            pe.wait_ge(y_ok, b * NT + c)
                        for h in range(NH):
                            i = pe.matmul(yb[:, h * HD:(h + 1) * HD], mt[:, c % 2, h], xs[:, c, h * HD:(h + 1) * HD],
                                          start=(h == 0), stop=True, skip_group_check=True)
                        if c:
                            pe.wait_ge(h_ok, b * (NT - 1) + c)
                            i = pe.matmul(yb[:, DI:2 * DI], cT[:, c * P:(c + 1) * P], state[:, (c - 1) % 2], start=False, stop=True,
                                          skip_group_check=True)
                        i.then_inc(y_ps, 1)
                        pe.wait_ge(scan_ok, b * 4 + c + 1)
                        pe.wait_ge(dbc_ok, b * 2 + 2)
                        if c >= 2:
                            pe.wait_ge(pk_ok, b * 4 + 4 + c - 1)
                        for t in range(NT):
                            i = pe.transpose(banks[2 + c % 2][:, t * P:(t + 1) * P], scan_out[:, c, t * P:(t + 1) * P], ident[:])
                        i.then_inc(scT_ps, 1)
                ahead(pe, first_half, both_halves)

            @block.scalar
            def _(act):
                own = Chain(act, act_own)
                nc.scalar.preload_act_table_set("natural_log_exp_and_others")

                def turned(b):
                    act.wait_ge(xnT_ps, b + 1)
                    act.wait_ge(xnT_all, b + 1)
                    nc.scalar.copy(xnc[:], banks[0][:]).then_inc(xnT_ok, 1)
                    act.wait_ge(xhT_ps, b + 1)
                    nc.scalar.activation(xhT[:], banks[1][:], ACT.Identity, scale=ni[:, 0:1], bias=ni[:, 1:2]).then_inc(xhT_ok, 1)

                def first_half(b):
                    rsqrt_by_exp(nc, act, own, nm1, var1, rs1, b + 1)
                    rsqrt_by_exp(nc, act, own, nm2, var2, rs2, b + 1)
                    act.wait_ge(mix_ex, 1)
                    nc.scalar.activation(mix_w[:, 4:6], mix_w[:, 2:4], ACT.Exp).then_inc(mix_ex, 1)
                    act.wait_ge(wts, 16 * 14)
                    own.now(nc.scalar.activation(neg_a[:], head_rows[:, 0], ACT.Exp))
                    own.now(nc.scalar.mul(neg_a[:], neg_a[:], -1.0))
                    turned(b)

                def both_halves(b, nxt):
                    own.base, own.n = b * 2 + 4, 0

                    def zx_out(t):
                        act.wait_ge(zx_ps, b * NT + t + 1)
                        nc.scalar.copy(z_all[:, bass.ds(b * NT + t, 1)].rearrange("p a d -> p (a d)"),
                                       banks[t][:, 0:DI]).then_inc(zx_ok, 1)
                        nc.scalar.copy(xs[:, t], banks[t][:, DI:]).then_inc(zx_ok, 1)

                    if nxt is not None:
                        rsqrt_by_exp(nc, act, own, nm1, var1, rs1, nxt + 1)
                    act.wait_ge(spilled, b * 48 + 16)
                    for j in range(2):
                        act.wait_ge(bcd_ps, b * 2 + j + 1)
                        nc.scalar.copy(bcd[:, 2 * j:2 * j + 2], banks[4 + j][:].rearrange("p (a n) -> p a n", a=2)[:, :, 0:2 * NS + NH]).then_inc(bcd_ok, 1)
                    zx_out(0)
                    zx_out(1)
                    act.wait_ge(dt_v, b + 1)
                    nc.scalar.activation(dt_w[:, 1], dt_w[:, 0], ACT.Exp).then_inc(dt_e, 1)
                    act.wait_ge(dt_u, b + 1)
                    nc.scalar.activation(dt_w[:, 3], dt_w[:, 2], ACT.Ln).then_inc(dt_l, 1)
                    zx_out(2)
                    act.wait_ge(dt_w_ok, b + 1)
                    nc.scalar.activation(dt_w[:, 9], dt_w[:, 8], ACT.Exp).then_inc(dt_x, 1)
                    zx_out(3)
                    act.wait_ge(rt_sh, b + 1)
                    nc.scalar.activation(rt.ex[:], rt.sh[:], ACT.Exp).then_inc(rt_ex, 1)
                    for j, k in ((0, 0), (1, 1)):
                        act.wait_ge(em_ps, b * 4 + j + 1)
                        nc.scalar.copy(xT[:, j], banks[k][:]).then_inc(em_ok, 1)
                    for j, k in ((0, 0), (1, 1)):
                        nc.scalar.activation(xT2[:, j], banks[k][:], ACT.Square).then_inc(em_ok, 1)
                    act.wait_ge(em_ps, b * 4 + 3)
                    nc.scalar.copy(bT[:], banks[6][:]).then_inc(em_ok, 1)
                    nc.scalar.activation(bT2[:], banks[6][:], ACT.Square).then_inc(em_ok, 1)
                    act.wait_ge(em_ps, b * 4 + 4)
                    nc.scalar.copy(cT[:], banks[7][:]).then_inc(em_ok, 1)
                    if nxt is not None:
                        rsqrt_by_exp(nc, act, own, nm2, var2, rs2, nxt + 1)
                    act.wait_ge(cum_ps, b + 1)
                    nc.scalar.activation(e_ct[:].rearrange("p a t h -> p (a t h)"), banks[4][:, 0:2 * NT * NH],
                                         ACT.Exp).then_inc(ect_ok, 1)
                    act.wait_ge(ncum_ok, b + 1)
                    nc.scalar.activation(e_tail[:], tail[:], ACT.Exp).then_inc(etail_ok, 1)
                    for half in range(2):
                        act.wait_ge(dbc_ps, b * 2 + half + 1)
                        nc.scalar.copy(dec_bc[:, half], banks[2 + half][:]).then_inc(dbc_ok, 1)
                    for c in range(NT):
                        if c == 1:
                            act.wait_ge(g_ps, b + 1)
                            nc.scalar.copy(gram[:], banks[5][:]).then_inc(g_ok, 1)
                        act.wait_ge(l_ps, b * NT + c + 1)
                        if c >= 2:
                            act.wait_ge(m_ok, b * NT + c - 1)
                        for h in range(NH):
                            i = nc.scalar.activation(lmat[:, c % 2, h], banks[c % 2][:, h * P:(h + 1) * P], ACT.Exp,
                                                     bias=ncum[:, c, h:h + 1])
                        i.then_inc(l_ok, 1)
                    if nxt is not None:
                        turned(nxt)
                        assert own.n == 2
                ahead(act, first_half, both_halves)
            @block.vector
            def _(dve):
                own = Chain(dve, dve_own)
                dve.sem_inc(y_ok, 1)
                dve.sem_inc(pk_ok, 4)
                own.now(nc.vector.memset(rt.masked_out[:], 3e38))
                own1 = Chain(dve, dve_own1)
                x_tile = lambda b, t: x1[:, bass.ds(b * NT + t, 1)].rearrange("p a d -> p (a d)")

                def norms(b, step):
                    if step == 0:
                        own1.base, own1.n = b * DVE_A1, 0
                        norm_stats(nc, dve, own1, stats_ok, nm1, lambda t: x_tile(b, t), var1)
                    if step == 1:
                        norm_apply(nc, dve, own1, nm1, lambda t: x_tile(b, t), xn, rs1, b + 1)
                        dve.sem_inc(xn_ok, 1)
                    if step == 2:
                        norm_stats(nc, dve, own1, stats_ok, nm2, lambda t: xn[:, t], var2)
                    if step == 3:
                        norm_apply(nc, dve, own1, nm2, lambda t: xn[:, t], xh, rs2, b + 1)
                        dve.sem_inc(xh_ok, 1)
                        assert own1.n == DVE_A1, own1.n

                def first_half(b):
                    for step in range(4):
                        norms(b, step)

                def both_halves(b, nxt):
                    own.base, own.n = b * DVE_A2 + first, 0
                    if nxt is not None:
                        norms(nxt, 0)
                        norms(nxt, 1)
                    dve.wait_ge(bcd_ok, b * 2 + 2)
                    w = lambda j: dt_w[:, j]
                    own.now(nc.vector.tensor_tensor(w(0), bcd[:, :, 2 * NS:], head_rows[:, 1].unsqueeze(1).broadcast_to([P, NT, NH]), ALU.add))
                    nc.vector.tensor_scalar(w(0), w(0), 0.0, None, ALU.min).then_inc(dt_v, 1)
                    dve.wait_ge(dt_e, b + 1)
                    nc.vector.tensor_scalar(w(2), w(1), 1.0, None, ALU.add).then_inc(dt_u, 1)
                    dve.wait_ge(dt_u, b + 1)
                    own.now(nc.vector.tensor_scalar(w(4), w(2), -1.0, 1e-30, ALU.add, ALU.max))
                    own.now(nc.vector.reciprocal(w(5), w(4)))
                    own.now(nc.vector.tensor_tensor(w(6), w(1), w(5), ALU.mult))
                    dve.wait_ge(dt_l, b + 1)
                    own.now(nc.vector.tensor_tensor(w(7), w(3), w(6), ALU.mult))
                    own.now(nc.vector.tensor_scalar(w(7), w(7), 0.001, 0.1, ALU.max, ALU.min))
                    nc.vector.tensor_tensor(w(8), w(7), neg_a[:].unsqueeze(1).broadcast_to([P, NT, NH]), ALU.mult).then_inc(dt_w_ok, 1)
                    dve.wait_ge(dt_w_ok, b + 1)
                    nc.vector.tensor_scalar(la[:], w(8), LOG_MAX_DECAY, None, ALU.min).then_inc(la_ok, 1)
                    dve.wait_ge(dt_x, b + 1)
                    nc.vector.tensor_scalar(decay[:], w(9), 0.99, None, ALU.min).then_inc(decay_ok, 1)
                    dve.wait_ge(rt_ps, b + 1)
                    choose_two(nc, dve, own, stats_ok, rt, banks[5][:, 0:NT * E].rearrange("p (t e) -> p t e", e=E), router_b,
                               rt_done, rt_sh, b + 1)
                    i = weigh_two(nc, dve, own, rt, rt_ex, b + 1, cw_all[:, bass.ds(b * NT, NT)])
                    if nxt is not None:
                        norms(nxt, 2)
                    dve.wait_ge(cum_ps, b + 1)
                    dve.wait_ge(ect_ok, b + 1)
                    cum = banks[4][:, 0:NT * NH].rearrange("p (t h) -> p t h", t=NT)
                    tot = banks[4][:, NT * NH:2 * NT * NH].rearrange("p (t h) -> p t h", t=NT)
                    own.now(nc.vector.tensor_scalar(ncum[:], cum, -1.0, None, ALU.mult))
                    nc.vector.tensor_tensor(tail[:], tot, ncum[:], ALU.add).then_inc(ncum_ok, 1)

                    def masked_product(c):
                        dve.wait_ge(l_ok, b * NT + c + 1)
                        g = gram[:, c * P:(c + 1) * P].unsqueeze(1).broadcast_to([P, NH, P])
                        if c >= 2:
                            dve.wait_ge(y_ps, b * NT + c - 1)
                        nc.vector.scalar_tensor_tensor(mt[:, c % 2], lmat[:, c % 2], 0.5, g, ALU.mult, ALU.mult).then_inc(m_ok, 1)

                    def peak_of(k):
                        dve.wait_ge(scT_ps, b * 4 + k + 1)
                        nc.vector.tensor_reduce(pk[:, k], banks[2 + k % 2][:].rearrange("p (t n) -> p t n", n=HD), AX,
                                                ALU.max).then_inc(pk_ok, 1)
                        if k % 2:
                            dve.wait_ge(pk_ok, b * 4 + 4 + k + 1)
                            own.did(nc.vector.tensor_tensor(peak[:, bass.ds(b, 1), k // 2].rearrange("p a c -> p (a c)"),
                                                            pk[:, k - 1], pk[:, k], ALU.mult))

                    def decayed_sums(c):
                        half = c // 2
                        dve.wait_ge(dbc_ok, b * 2 + half + 1)
                        dve.wait_ge(em_ok, b * 7 + 6)
                        nc.vector.tensor_tensor_scan(scan_out[:, c], dec_bc[:, half], bT2[:] if c % 2 else xT2[:, half], 0.0,
                                                     ALU.mult, ALU.add).then_inc(scan_ok, 1)

                    if nxt is not None:
                        norms(nxt, 3)
                    decayed_sums(0)
                    decayed_sums(1)
                    dve.wait_ge(g_ok, b + 1)
                    masked_product(0)
                    for c in range(NT):
                        if c < 2:
                            decayed_sums(c + 2)
                        if c + 1 < NT:
                            masked_product(c + 1)
                        if c < NT - 1:
                            dve.wait_ge(h_ps, b * (NT - 1) + c + 1)
                            for h in range(NH):
                                rows, cols = slice(NS * (h // 2), NS * (h // 2 + 1)), slice(h * HD, (h + 1) * HD)
                                st, up = state[rows, c % 2, cols], banks[4 + c % 2][rows, cols]
                                if c == 0:
                                    i = own.did(nc.vector.tensor_copy(st, up))
                                else:
                                    i = own.did(nc.vector.scalar_tensor_tensor(st, state[rows, (c - 1) % 2, cols],
                                                                               e_ct[rows, 1, c, h:h + 1], up, ALU.mult, ALU.add))
                            own.after(i)
                            dve.sem_inc(h_ok, 1)
                        dve.wait_ge(y_ps, b * NT + c + 1)
                        dve.wait_ge(xd_ok, b * NT + c + 1)
                        yb = banks[6 + c % 2]
                        dst = y_all[:, bass.ds(b * NT + c, 1)].rearrange("p a d -> p (a d)")
                        intra = lambda to: nc.vector.tensor_tensor(to, yb[:, 0:DI], xd[:, c].rearrange("p h d -> p (h d)"), ALU.add)
                        if c:
                            dve.wait_ge(y_ok, b * NT + c + 1)
                            own.did(intra(yt[:, 0]))
                            own.now(nc.vector.tensor_tensor(yt[:, 1].rearrange("p (h d) -> p h d", h=NH),
                                                    yb[:, DI:].rearrange("p (h d) -> p h d", h=NH),
                                                    e_ct[:, 0, c].unsqueeze(2).broadcast_to([P, NH, HD]), ALU.mult))
                            nc.vector.tensor_tensor(dst, yt[:, 0], yt[:, 1], ALU.add).then_inc(y_ok, 1)
                        else:
                            intra(dst).then_inc(y_ok, 1)
                        peak_of(c)
                    assert own.n == DVE_A2, own.n

                dve.wait_ge(x_first, 16)
                first_half(0)
                dve.wait_ge(wts_m, 32)
                own.now(nc.vector.tensor_scalar(dp[:], dp[:], 0.01, 0.9999, ALU.max, ALU.min))
                own.now(nc.vector.tensor_reduce(mix_w[:, 0:1], mix[:], AX, ALU.max))
                nc.vector.tensor_scalar(mix_w[:, 2:4], mix[:], mix_w[:, 0:1], None, ALU.subtract).then_inc(mix_ex, 1)
                dve.wait_ge(mix_ex, 2)
                own.now(nc.vector.tensor_reduce(mix_w[:, 1:2], mix_w[:, 4:6], AX, ALU.add))
                own.now(nc.vector.reciprocal(mix_w[:, 1:2], mix_w[:, 1:2]))
                own.now(nc.vector.tensor_scalar(mix_w[:, 6:8], mix_w[:, 4:6], mix_w[:, 1:2], AD ** -0.5, ALU.mult, ALU.mult))
                own.now(nc.vector.memset(powers[:], 1.0))
                own.now(nc.vector.memset(table[:], 1.0))
                for n in range(2):
                    own.now(nc.vector.tensor_tensor_scan(powers[:, n, 1:S], dp[:, n:n + 1].broadcast_to([AH, S - 1]),
                                                         table[:, 1:S], 1.0, ALU.mult, ALU.mult))
                own.now(nc.vector.tensor_scalar(powers[:, 0], powers[:, 0], mix_w[:, 6:7], None, ALU.mult))
                nc.vector.scalar_tensor_tensor(table[:], powers[:, 1], mix_w[:, 7:8], powers[:, 0], ALU.mult,
                                               ALU.add).then_inc(table_ok, 1)
                dve.wait_ge(table_ok, 1)
                tb = table[:]
                nc.vector.tensor_copy(table_r[:], bass.AP(tensor=tb.tensor, offset=tb.offset + S - 1,
                                                          ap=[list(tb.ap[0]), [-1, S]])).then_inc(table_ok, 1)
                first = own.n
                dve.wait_ge(consts, 3)
                dve.wait_ge(x_rest, 16)
                with dve.Fori(0, NB - 1) as b:
                    both_halves(b, b + 1)
                both_halves(NB - 1, None)

        with ExitStack() as work:
            wb = in_scope(work)
            STEPS = 32
            peak1 = wb("peak1", [P, 1])
            peak_all = wb("peak_all", [P, 1])
            safe = wb("safe", [P, 1], I32)
            x_steps = wb("x_steps", [P, 2, S])
            d_steps = wb("d_steps", [P, 2, S])
            y_steps = wb("y_steps", [P, 2, S])
            bc_steps = wb("bc_steps", [P, STEPS, 2 * NS])
            d_col = wb("d_col", [P, 2])
            h_st = wb("h_st", [P, 2, NS])
            h_in = wb("h_in", [P, 2, NS])
            names = ("peak1", "peak_all", "safe", "x_in", "bc_in", "bc_used", "own", "y_ok", "yT_ps", "y_used", "d_in", "gap")
            G = {n: sem("f_" + n) for n in names}
            block = work.enter_context(nc.Block())

            @block.gpsimd
            def _(pool):
                pool.wait_ge(G["peak1"], 1)
                nc.gpsimd.partition_all_reduce(peak_all[:], peak1[:], P, bass.bass_isa.ReduceOp.max).then_inc(G["peak_all"], 1)

            @block.sync
            def _(sp):
                for h in range(NH):
                    dst = d_col[HD * (h % 2):HD * (h % 2 + 1), h // 2:h // 2 + 1]
                    d_h = ins["Dparam"]
                    sp.dma_start(dst, bass.AP(tensor=d_h.tensor, offset=d_h.offset + h, ap=[[0, HD], [1, 1]])).then_inc(G["d_in"], 16)
                sp.wait_ge(G["d_in"], 16 * NH)
                sp.wait_ge(G["safe"], 1)
                all_safe = sp.value_load(safe[0:1, 0:1], min_val=0, max_val=1)
                with sp.If(all_safe == 0):
                    sp.sem_inc(G["bc_used"], 1)
                    with sp.Fori(0, NB) as b:
                        sp.wait_ge(G["y_used"], b + 1)
                        sp.dma_start(x_steps[:], xT_d[bass.ds(b, 1)].rearrange("a p h s -> p (a h) s")).then_inc(G["x_in"], 16)
                        sp.dma_start(d_steps[:], dec_d[bass.ds(b, 1)].rearrange("a p h s -> p (a h) s")).then_inc(G["x_in"], 16)
                        with sp.Fori(0, S // STEPS) as c:
                            sp.wait_ge(G["bc_used"], b * (S // STEPS) + c + 1)
                            src = bc_d.rearrange("b t p n -> (b t p) n")[bass.ds(b * S + c * STEPS, STEPS)]
                            sp.dma_start(bc_steps[:], src.partition_broadcast(P)).then_inc(G["bc_in"], 16)
                with sp.Else():
                    sp.nop()

            @block.tensor
            def _(pe):
                pe.wait_ge(G["safe"], 1)
                all_safe = pe.value_load(safe[0:1, 0:1], min_val=0, max_val=1)
                with pe.If(all_safe == 0):
                    with pe.Fori(0, NB) as b:
                        pe.wait_ge(G["y_ok"], b + 1)
                        for t in range(NT):
                            for half in range(2):
                                i = pe.transpose(banks[t][:, half * P:(half + 1) * P], y_steps[:, half, t * P:(t + 1) * P], ident[:])
                        i.then_inc(G["yT_ps"], 1)
                with pe.Else():
                    pe.nop()

            @block.vector
            def _(dve):
                nc.vector.tensor_reduce(peak1[:], peak[:].rearrange("p b a c -> p (b a c)"), AX, ALU.max).then_inc(G["peak1"], 1)
                dve.wait_ge(G["peak_all"], 1)
                nc.vector.tensor_scalar(safe[:], peak_all[:], SAFE, None, ALU.is_le).then_inc(G["safe"], 1)
                dve.wait_ge(G["safe"], 1)
                all_safe = dve.value_load(safe[0:1, 0:1], min_val=0, max_val=1)
                with dve.If(all_safe == 0):
                    own = Chain(dve, G["own"])
                    dve.sem_inc(G["y_used"], 1)
                    dve.wait_ge(G["d_in"], 16 * NH)
                    dve.sem_inc(G["gap"], 1)
                    PER_STEP, PER_SEQ = 6, 6 * S + 1 + 2 + NT
                    with dve.Fori(0, NB) as b:
                        own.base, own.n = b * PER_SEQ, 0
                        own.now(nc.vector.memset(h_st[:], 0.0))
                        dve.wait_ge(G["x_in"], b * 32 + 32)
                        dve.sem_inc(G["gap"], 1)
                        with dve.Fori(0, S // STEPS) as c:
                            dve.wait_ge(G["bc_in"], (b * (S // STEPS) + c + 1) * 16)
                            dve.sem_inc(G["gap"], 1)
                            with dve.Fori(0, STEPS) as s:
                                t = c * STEPS + s
                                own.base, own.n = b * PER_SEQ + 1 + t * PER_STEP, 0
                                at = lambda x: x[:, :, bass.ds(t, 1)].broadcast_to([P, 2, NS])
                                bc = lambda k: bc_steps[:, bass.ds(s, 1), k * NS:(k + 1) * NS].broadcast_to([P, 2, NS])
                                own.now(nc.vector.tensor_tensor(h_st[:], h_st[:], at(d_steps), ALU.mult))
                                own.now(nc.vector.tensor_tensor(h_in[:], bc(0), at(x_steps), ALU.mult))
                                own.now(nc.vector.tensor_tensor(h_st[:], h_st[:], h_in[:], ALU.add))
                                own.now(nc.vector.tensor_scalar(h_st[:], h_st[:], -CLIP, CLIP, ALU.max, ALU.min))
                                own.now(nc.vector.tensor_tensor(h_in[:], h_st[:], bc(1), ALU.mult))
                                own.now(nc.vector.tensor_reduce(y_steps[:, :, bass.ds(t, 1)], h_in[:], AX, ALU.add))
                            dve.sem_inc(G["bc_used"], 1)
                        own.base, own.n = b * PER_SEQ + 1 + S * PER_STEP, 0
                        for half in range(2):
                            i = own.did(nc.vector.scalar_tensor_tensor(y_steps[:, half], x_steps[:, half], d_col[:, half:half + 1],
                                                                       y_steps[:, half], ALU.mult, ALU.add))
                        own.after(i)
                        dve.sem_inc(G["y_ok"], 1)
                        dve.wait_ge(G["yT_ps"], b + 1)
                        for t in range(NT):
                            i = own.did(nc.vector.tensor_copy(y_all[:, bass.ds(b * NT + t, 1)].rearrange("p a d -> p (a d)"),
                                                              banks[t][:, 0:DI]))
                        own.after(i)
                        dve.sem_inc(G["y_used"], 1)
                with dve.Else():
                    dve.nop()

        with ExitStack() as work:
            wb = in_scope(work)
            sg = wb("sg", [P, 2, S])
            eo = wb("eo", [P, 2, 2, S])
            cw = wb("cw", [P, NT, E])
            (g_ps2, u_ps, sg_ok, eo_ok, o_ps, o_ok, zs_ok, gate_ok, own_b, gap_b) = (
                sem(n) for n in ("g_ps2", "u_ps", "sg_ok", "eo_ok", "o_ps", "o_ok", "zs_ok", "gate_ok", "own_b", "gap_b"))
            NK = 2 * (1 + E)
            block = work.enter_context(nc.Block())

            @block.tensor
            def _(pe):
                pe.wait_ge(wts_b, 16 * 8)
                pe.sem_inc(o_ps, 2)
                with pe.Fori(0, NB) as b:
                    xT_b = xnT[:, bass.ds(b, 1)].rearrange("p a s -> p (a s)")

                    def up(e):
                        for m in range(2):
                            k = 2 * e + m
                            pe.wait_ge(eo_ok, b * NK + k + 1)
                            pe.matmul(banks[2 * (k % 2)][:], w13[:, e, 0, m * P:(m + 1) * P], xT_b,
                                      start=True, stop=True).then_inc(g_ps2, 1)
                            pe.matmul(banks[2 * (k % 2) + 1][:], w13[:, e, 1, m * P:(m + 1) * P], xT_b,
                                      start=True, stop=True).then_inc(u_ps, 1)

                    def down(e):
                        pe.wait_ge(eo_ok, b * NK + 2 * (e + 1) + 2)
                        pe.wait_ge(o_ok, b * (1 + E) + e + 1)
                        for t in range(NT):
                            for m in range(2):
                                i = pe.matmul(banks[4 + e % 2][:, t * P:(t + 1) * P], eo[:, e % 2, m, t * P:(t + 1) * P],
                                              w2[:, e, m], start=(m == 0), stop=(m == 1))
                        i.then_inc(o_ps, 1)

                    up(0)
                    for e in range(1 + E):
                        if e < E:
                            up(e + 1)
                        down(e)

            @block.scalar
            def _(act):
                nc.scalar.preload_act_table(ACT.Silu)
                with act.Fori(0, NB) as b:
                    for k in range(NK):
                        act.wait_ge(g_ps2, b * NK + k + 1)
                        act.wait_ge(eo_ok, b * NK + k + 1)
                        nc.scalar.activation(sg[:, k % 2], banks[2 * (k % 2)][:], ACT.Silu).then_inc(sg_ok, 1)
                        if k % 4 == 3:
                            zt = z_all[:, bass.ds(b * NT + k // 4, 1)].rearrange("p a d -> p (a d)")
                            nc.scalar.activation(zt, zt, ACT.Silu).then_inc(zs_ok, 1)

            @block.vector
            def _(dve):
                own = Chain(dve, own_b)
                dve.sem_inc(eo_ok, 2)
                dve.sem_inc(o_ok, 2)
                with dve.Fori(0, NB) as b:
                    own.base, own.n = b * DVE_B, 0
                    own.now(nc.vector.tensor_copy(cw[:], cw_all[:, bass.ds(b * NT, NT)]))

                    def combine(e):
                        dve.wait_ge(o_ps, b * (1 + E) + e + 1 + 2)
                        bank = banks[4 + e % 2]
                        if e == 0:
                            xb = x1[:, bass.ds(b * NT, NT)].rearrange("p t d -> p (t d)")
                            k = own.did(nc.vector.tensor_tensor(xb, bank[:], xb, ALU.add))
                        else:
                            for t in range(NT):
                                xt = x1[:, bass.ds(b * NT + t, 1)].rearrange("p a d -> p (a d)")
                                k = own.did(nc.vector.scalar_tensor_tensor(xt, bank[:, t * P:(t + 1) * P],
                                                                           cw[:, t, e - 1:e], xt, ALU.mult, ALU.add))
                        own.after(k)
                        dve.sem_inc(o_ok, 1)

                    def gated_stats(t):
                        dve.wait_ge(gate_ok, b * NT + t + 1)
                        dve.sem_inc(gap_b, 1)
                        tile = lambda x: x[:, bass.ds(b * NT + t, 1)].rearrange("p a d -> p (a d)")
                        own.did(nc.vector.bn_stats(tile(y_bn), tile(y_all)))

                    for k in range(NK):
                        e, m = k // 2, k % 2
                        dve.wait_ge(sg_ok, b * NK + k + 1)
                        dve.wait_ge(u_ps, b * NK + k + 1)
                        dve.wait_ge(o_ps, b * (1 + E) + e + 1)
                        nc.vector.tensor_tensor(eo[:, e % 2, m], sg[:, m], banks[2 * m + 1][:], ALU.mult).then_inc(eo_ok, 1)
                        if m and e:
                            combine(e - 1)
                        if k % 4 == 0 and k:
                            t = k // 4 - 1
                            dve.wait_ge(zs_ok, b * NT + t + 1)
                            yt_ = y_all[:, bass.ds(b * NT + t, 1)].rearrange("p a d -> p (a d)")
                            zt = z_all[:, bass.ds(b * NT + t, 1)].rearrange("p a d -> p (a d)")
                            nc.vector.tensor_tensor(yt_, yt_, zt, ALU.mult).then_inc(gate_ok, 1)
                        if k % 4 == 2 and k > 4:
                            gated_stats(k // 4 - 1)
                    gated_stats(NT - 1)
                    combine(E)
                    assert own.n == DVE_B, own.n

        early.close()
        sb_late = in_scope(ctx)
        mask = sb_late("mask", [P, AH, MW])
        v3 = sb_late("v3", [P, TT, 3, DM], BF16)
        NP = 9 * AD
        qx = sb_late("qx", [NP, 2, S], BF16)
        kx = sb_late("kx", [NP, 2, S], BF16)
        qk_in = [sem("qk_in0"), sem("qk_in1")]

        def load_qk(sp, h, g, j):
            for i in range(3):
                for dst, part, rows in ((qx, 0, slice(i, i + 1)), (kx, 1, slice(0, 3))):
                    src = parts_d[part, rows, bass.ds(g * 2 + j, 1), bass.ds(h * AD, AD)]
                    src = src.rearrange("i a d s -> i (a d) s")
                    if part == 0:
                        src = src.broadcast_to([3, AD, S])
                    sp.dma_start(dst[3 * AD * i:3 * AD * (i + 1), j], src).then_inc(qk_in[j], 16)

        with ExitStack() as work:
            wb = in_scope(work)
            nmo, nmx = Norm(wb, "nmo"), Norm(wb, "nmx")
            y_mv = wb("y_mv", [P, TT, 2])
            y_rs = wb("y_rs", [P, 4, TT])
            y_mr = wb("y_mr", [P, NT, 2])
            yn = wb("yn", [P, NT, DI])
            yT = wb("yT", [P, 2, S])
            oc = wb("oc", [P, NT, DM])
            on = wb("on", [P, NT, DM])
            x2n = wb("x2n", [P, NT, DM])
            x2T = wb("x2T", [P, S])
            qk = wb("qk", [P, 2, S])
            vt = wb("vt", [P, NT, DM])
            gw = wb("gw", [P, NT, E])
            gwT = wb("gwT", [E, S])
            onw = wb("onw", [P, NT, DM])
            onb = wb("onb", [P, NT, DM])
            parts = wb("parts", [P, 3, 2, S], BF16)
            rest = wb("rest", [P, 2, S])
            vrest = wb("vrest", [P, NT, DM])
            rt2 = Router(wb, "rt2")
            names = ("vy", "ry", "vo", "ro", "vx", "rx", "yn_ok", "yT_ps", "yT_ok", "out_ps", "out_ok", "on_ok", "aff_ok",
                     "x2_ok", "x2T_ps", "x2T_ok", "lg_ps", "lg_ok", "sh_ok", "ex_ok", "gw_ok", "gwT_ps", "gwT_ok", "bias_ps",
                     "bias_ok", "ex_ps", "mix_ok", "qk_ps", "qk_ok", "rest_ok", "p2_ok", "split_ok", "kept", "v_ps", "v_ok",
                     "v1_ok", "vrest_ok", "v2_ok", "v3_ok", "own_y", "own_1", "own_2", "own_ac", "own_g", "own_p")
            C = {n: sem("c_" + n) for n in names}
            block = work.enter_context(nc.Block())

            @block.sync
            def _(sp):
                sp.wait_ge(mirrored, 32)
                for h in range(AH):
                    src = bass.AP(tensor=mirror_d.tensor, offset=mirror_d.offset + h * 2 * S,
                                  ap=[[1, P], [1, MW]])
                    sp.dma_start(mask[:, h], src).then_inc(mask_in, 16)
                sp.sem_inc(C["kept"], 16)

                def keep(b):
                    sp.wait_ge(C["split_ok"], b + 2)
                    for j in range(2):
                        for i in range(3):
                            sp.dma_start(parts_d[j, i, bass.ds(b, 1)].rearrange("a p s -> p (a s)"),
                                         parts[:, i, j]).then_inc(C["kept"], 16)

                keep(0)
                keep(1)
                sp.wait_ge(C["kept"], 16 + 6 * 16 * 2)
                load_qk(sp, 0, 0, 0)
                load_qk(sp, 0, 0, 1)
                with sp.Fori(2, NB) as b:
                    keep(b)
                sp.wait_ge(C["kept"], 16 + 6 * 16 * NB)
                sp.wait_ge(mask_in, 16 * AH)

            def staged(eng, start, stages):
                start()
                with eng.Fori(0, NB - 2) as b:
                    stages(b, b + 1, b + 2)
                stages(NB - 2, NB - 1, None)
                stages(NB - 1, None, None)

            @block.gpsimd
            def _(pool):
                def affine(b):
                    pool.wait_ge(C["on_ok"], b + 1)
                    rows = lambda j: no_rows[:, j].unsqueeze(1).broadcast_to([P, NT, DM])
                    nc.gpsimd.tensor_tensor(onw[:], on[:], rows(0), ALU.mult).then_inc(C["own_p"], 1)
                    pool.wait_ge(C["own_p"], b + 1)
                    nc.gpsimd.tensor_tensor(onb[:], onw[:], rows(1), ALU.add).then_inc(C["aff_ok"], 1)

                def stages(b, nxt, nxt2):
                    if nxt is not None:
                        affine(nxt)
                    pool.wait_ge(C["qk_ok"], b * 4 + 4)
                    pool.wait_ge(C["split_ok"], b + 1)
                    nc.gpsimd.tensor_tensor(rest[:], qk[:], parts[:, 0], ALU.subtract).then_inc(C["rest_ok"], 1)
                    pool.wait_ge(C["v1_ok"], b + 1)
                    pool.wait_ge(C["v3_ok"], b + 1)
                    nc.gpsimd.tensor_tensor(vrest[:], vt[:], v3[:, bass.ds(b * NT, NT), 0], ALU.subtract).then_inc(C["vrest_ok"], 1)
                    pool.wait_ge(C["p2_ok"], b + 1)
                    nc.gpsimd.tensor_tensor(parts[:, 2], rest[:], parts[:, 1], ALU.subtract).then_inc(C["split_ok"], 1)
                    pool.wait_ge(C["v2_ok"], b + 1)
                    nc.gpsimd.tensor_tensor(v3[:, bass.ds(b * NT, NT), 2], vrest[:], v3[:, bass.ds(b * NT, NT), 1],
                                            ALU.subtract).then_inc(C["v3_ok"], 1)

                pool.sem_inc(C["split_ok"], 1)
                pool.sem_inc(C["v3_ok"], 1)
                staged(pool, lambda: affine(0), stages)

            @block.tensor
            def _(pe):
                def y_turned(b):
                    pe.wait_ge(C["yn_ok"], b + 1)
                    for half in range(2):
                        for t in range(NT):
                            i = pe.transpose(banks[4 + half][:, t * P:(t + 1) * P], yn[:, t, half * P:(half + 1) * P], ident[:])
                        i.then_inc(C["yT_ps"], 1)

                def out_proj(b):
                    pe.wait_ge(C["yT_ok"], b * 2 + 2)
                    for t in range(NT):
                        for half in range(2):
                            i = pe.matmul(banks[7][:, t * P:(t + 1) * P], yT[:, half, t * P:(t + 1) * P], wo[:, half],
                                          start=(half == 0), stop=(half == 1))
                    i.then_inc(C["out_ps"], 1)

                def start():
                    y_turned(0)
                    out_proj(0)

                def experts(b, pair, j):
                    pe.wait_ge(C["mix_ok"], b * 4 + 2 * pair + j + 1)
                    for t in (2 * pair, 2 * pair + 1):
                        i = pe.matmul(banks[2 * (t % 2) + j][:], x2T[:, t * P:(t + 1) * P],
                                      ew[:, 4 * j:4 * j + 4].rearrange("p e o -> p (e o)"), start=True, stop=True)
                    i.then_inc(C["ex_ps"], 1)

                def stages(b, nxt, nxt2):
                    pe.wait_ge(C["x2_ok"], b + 1)
                    for t in range(NT):
                        i = pe.transpose(banks[6][:, t * P:(t + 1) * P], x2n[:, t], ident[:])
                    i.then_inc(C["x2T_ps"], 1)
                    pe.wait_ge(C["bias_ok"], b + 1)
                    if nxt is not None:
                        y_turned(nxt)
                    pe.wait_ge(C["x2T_ok"], b + 1)
                    for t in range(NT):
                        i = pe.matmul(banks[6][:, t * E:(t + 1) * E], x2T[:, t * P:(t + 1) * P], gate_w[:], start=True, stop=True)
                    i.then_inc(C["lg_ps"], 1)
                    pe.wait_ge(C["v_ok"], b + 1)
                    pe.wait_ge(C["out_ok"], b + 1)
                    if nxt is not None:
                        out_proj(nxt)
                    for j in range(2):
                        pe.matmul(banks[4 + j][:], wqkv[:, j], x2T[:], start=True, stop=True).then_inc(C["qk_ps"], 1)
                    experts(b, 0, 0)
                    if nxt is not None:
                        pe.wait_ge(C["out_ok"], nxt + 1)
                    for t in range(NT):
                        i = pe.matmul(banks[7][:, t * P:(t + 1) * P], x2T[:, t * P:(t + 1) * P], wqkv[:, 2], start=True, stop=True)
                    i.then_inc(C["v_ps"], 1)
                    pe.wait_ge(C["qk_ok"], b * 4 + 4)
                    pe.wait_ge(C["gw_ok"], b + 1)
                    for t in range(NT):
                        i = pe.transpose(banks[4][0:E, t * P:(t + 1) * P], gw[:, t], ident[:])
                    i.then_inc(C["gwT_ps"], 1)
                    pe.wait_ge(C["gwT_ok"], b + 1)
                    for t in range(NT):
                        i = pe.matmul(banks[5][:, t * P:(t + 1) * P], gwT[:, t * P:(t + 1) * P], eb[:], start=True, stop=True)
                    i.then_inc(C["bias_ps"], 1)
                    experts(b, 0, 1)
                    experts(b, 1, 0)
                    experts(b, 1, 1)

                pe.wait_ge(wts_c, 16 * WTS_C)
                staged(pe, start, stages)

            @block.scalar
            def _(act):
                own = Chain(act, C["own_ac"])

                def y_turned(b):
                    for half in range(2):
                        act.wait_ge(C["yT_ps"], b * 2 + half + 1)
                        nc.scalar.activation(yT[:, half], banks[4 + half][:], ACT.Identity, scale=ln_cols[:, 0, half:half + 1],
                                             bias=ln_cols[:, 1, half:half + 1]).then_inc(C["yT_ok"], 1)

                o_rsqrt = lambda b: rsqrt_by_exp(nc, act, own, nmo, C["vo"], C["ro"], b + 1)
                x_rsqrt = lambda b: rsqrt_by_exp(nc, act, own, nmx, C["vx"], C["rx"], b + 1)

                def start():
                    own.base, own.n = 0, 0
                    act.wait_ge(C["vy"], 1)
                    own.now(nc.scalar.activation(y_rs[:, 1], y_rs[:, 0], ACT.Ln))
                    nc.scalar.activation(y_rs[:, 2], y_rs[:, 1], ACT.Exp, scale=-0.5).then_inc(C["ry"], 1)
                    y_turned(0)
                    o_rsqrt(0)
                    x_rsqrt(0)

                def stages(b, nxt, nxt2):
                    own.base, own.n = b * 2 + 3, 0
                    act.wait_ge(C["x2T_ps"], b + 1)
                    nc.scalar.copy(x2T[:], banks[6][:]).then_inc(C["x2T_ok"], 1)
                    if nxt is not None:
                        y_turned(nxt)
                    act.wait_ge(C["sh_ok"], b + 1)
                    nc.scalar.activation(rt2.ex[:], rt2.sh[:], ACT.Exp).then_inc(C["ex_ok"], 1)
                    if nxt is not None:
                        o_rsqrt(nxt)
                    act.wait_ge(C["rest_ok"], b + 1)
                    act.wait_ge(C["kept"], b * 96 + 16)
                    for j in range(2):
                        act.wait_ge(C["qk_ps"], b * 2 + j + 1)
                        for dst in (qk[:, j], parts[:, 0, j]):
                            nc.scalar.activation(dst, banks[4 + j][:], ACT.Identity, bias=bqk[:, j:j + 1]).then_inc(C["qk_ok"], 1)
                    act.wait_ge(C["gwT_ps"], b + 1)
                    nc.scalar.copy(gwT[:], banks[4][0:E, :]).then_inc(C["gwT_ok"], 1)
                    act.wait_ge(C["v_ok"], b + 2)
                    v_b = v3[:, bass.ds(b * NT, NT)]
                    nc.scalar.copy(v_b[:, :, 0], vt[:]).then_inc(C["v1_ok"], 1)
                    if nxt is not None:
                        x_rsqrt(nxt)
                    act.wait_ge(C["rest_ok"], b + 2)
                    nc.scalar.copy(parts[:, 1], rest[:]).then_inc(C["p2_ok"], 1)
                    act.wait_ge(C["vrest_ok"], b + 2)
                    nc.scalar.copy(v_b[:, :, 1], vrest[:]).then_inc(C["v2_ok"], 1)

                nc.scalar.preload_act_table_set("natural_log_exp_and_others")
                act.wait_ge(wts_c, 16 * WTS_C)
                staged(act, start, stages)

            @block.vector
            def _(dve):
                own_y, own1, own2 = (Chain(dve, C[n]) for n in ("own_y", "own_1", "own_2"))
                gap = C["own_g"]
                tile_of = lambda x, b, t: x[:, bass.ds(b * NT + t, 1)].rearrange("p a d -> p (a d)")
                tiles_of = lambda x, b: x[:, bass.ds(b * NT, NT)]

                def y_rstd():
                    dve.sem_inc(gap, 1)
                    for t in range(TT):
                        i = own_y.did(nc.vector.bn_aggr(y_mv[:, t], y_bn[:, t]))
                    own_y.after(i)
                    nc.vector.tensor_scalar(y_rs[:, 0], y_mv[:, :, 1], EPS, None, ALU.add).then_inc(C["vy"], 1)
                    dve.wait_ge(C["ry"], 1)
                    own_y.now(nc.vector.tensor_tensor(y_rs[:, 3], y_rs[:, 2], y_rs[:, 0], ALU.mult))
                    own_y.now(nc.vector.tensor_tensor(y_rs[:, 3], y_rs[:, 3], y_rs[:, 2], ALU.mult))
                    own_y.now(nc.vector.tensor_scalar(y_rs[:, 3], y_rs[:, 3], -0.5, 1.5, ALU.mult, ALU.add))
                    own_y.now(nc.vector.tensor_tensor(y_mv[:, :, 1], y_rs[:, 3], y_rs[:, 2], ALU.mult))

                def y_apply(b):
                    own_y.base, own_y.n = b * DVE_CY + TT + 4, 0
                    own_y.now(nc.vector.tensor_copy(y_mr[:], tiles_of(y_mv, b)))
                    for t in range(NT):
                        i = own_y.did(nc.vector.tensor_scalar(yn[:, t], tile_of(y_all, b, t), y_mr[:, t, 0:1], y_mr[:, t, 1:2],
                                                              ALU.subtract, ALU.mult))
                    own_y.after(i)
                    dve.sem_inc(C["yn_ok"], 1)
                    assert own_y.n == DVE_CY, own_y.n

                def o_stats(b):
                    own1.base, own1.n = b * DVE_C1, 0
                    dve.wait_ge(C["out_ps"], b + 1)
                    nc.vector.tensor_scalar(oc[:].rearrange("p t d -> p (t d)"), banks[7][:], -CLIP, CLIP, ALU.max,
                                            ALU.min).then_inc(C["out_ok"], 1)
                    dve.wait_ge(C["out_ok"], b + 1)
                    norm_stats(nc, dve, own1, gap, nmo, lambda t: oc[:, t], C["vo"])

                def o_apply(b):
                    norm_apply(nc, dve, own1, nmo, lambda t: oc[:, t], on, C["ro"], b + 1)
                    dve.sem_inc(C["on_ok"], 1)

                def x_stats(b):
                    dve.wait_ge(C["aff_ok"], b + 1)
                    own1.now(nc.vector.tensor_tensor(tiles_of(x1, b), tiles_of(x1, b), onb[:], ALU.add))
                    norm_stats(nc, dve, own1, gap, nmx, lambda t: tile_of(x1, b, t), C["vx"])

                def x_apply(b):
                    norm_apply(nc, dve, own1, nmx, lambda t: tile_of(x1, b, t), x2n, C["rx"], b + 1)
                    dve.sem_inc(C["x2_ok"], 1)
                    assert own1.n == DVE_C1, own1.n

                def start():
                    y_rstd()
                    y_apply(0)
                    o_stats(0)
                    o_apply(0)
                    x_stats(0)
                    y_apply(1)
                    x_apply(0)

                def mixed(b, pair, half):
                    dve.wait_ge(C["ex_ps"], b * 4 + 2 * pair + half + 1)
                    for e in range(4 * half, 4 * half + 4):
                        for j in range(2):
                            t = 2 * pair + j
                            if e % 4:
                                own2.after(own2.n - 1)
                            xt = tile_of(x1, b, t)
                            i = own2.did(nc.vector.scalar_tensor_tensor(
                                xt, banks[2 * j + e // 4][:, (e % 4) * P:(e % 4 + 1) * P], gw[:, t, e:e + 1], xt, ALU.mult, ALU.add))
                    own2.after(i)
                    dve.sem_inc(C["mix_ok"], 1)

                def stages(b, nxt, nxt2):
                    own2.base, own2.n = b * DVE_C2 + 1, 0
                    dve.wait_ge(C["lg_ps"], b + 1)
                    choose_two(nc, dve, own2, gap, rt2, banks[6][:, 0:NT * E].rearrange("p (t e) -> p t e", e=E),
                               gate_b, C["lg_ok"], C["sh_ok"], b + 1)
                    if nxt is not None:
                        o_stats(nxt)
                    i = weigh_two(nc, dve, own2, rt2, C["ex_ok"], b + 1, gw[:])
                    own2.after(i)
                    dve.sem_inc(C["gw_ok"], 1)
                    if nxt is not None:
                        o_apply(nxt)
                    mixed(b, 0, 0)
                    dve.wait_ge(C["v_ps"], b + 1)
                    dve.wait_ge(C["vrest_ok"], b + 1)
                    nc.vector.tensor_tensor(vt[:], banks[7][:].rearrange("p (t d) -> p t d", t=NT),
                                            bv_row[:].unsqueeze(1).broadcast_to([P, NT, DM]), ALU.add).then_inc(C["v_ok"], 1)
                    if nxt2 is not None:
                        y_apply(nxt2)
                    dve.wait_ge(C["bias_ps"], b + 1)
                    nc.vector.tensor_tensor(tiles_of(x1, b), banks[5][:].rearrange("p (t d) -> p t d", t=NT), tiles_of(x1, b),
                                            ALU.add).then_inc(C["bias_ok"], 1)
                    dve.wait_ge(C["bias_ok"], b + 2)
                    if nxt is not None:
                        x_stats(nxt)
                    mixed(b, 0, 1)
                    if nxt is not None:
                        x_apply(nxt)
                    mixed(b, 1, 0)
                    mixed(b, 1, 1)
                    assert own2.n == DVE_C2, own2.n

                dve.wait_ge(wts_c, 16 * WTS_C)
                nc.vector.memset(rt2.masked_out[:], 3e38).then_inc(C["own_2"], 1)
                dve.wait_ge(C["own_2"], 1)
                dve.sem_inc(C["v_ok"], 1)
                dve.sem_inc(C["bias_ok"], 1)
                dve.sem_inc(C["mix_ok"], 2)
                dve.sem_inc(C["rest_ok"], 1)
                dve.sem_inc(C["vrest_ok"], 1)
                staged(dve, start, stages)

        att = sb_late("att", [P, TT, DM])
        with ExitStack() as work:
            wb = in_scope(work)
            m_cur = wb("m_cur", [P, MW])
            sm = wb("sm", [P, 4, S])
            pr = wb("pr", [P, 4, S])
            hi = wb("hi", [P, 4, S], F16)
            lo = wb("lo", [P, 4, S], F16)
            mx = wb("mx", [P, 4])
            nmx = wb("nmx", [P, 4])
            rsum = wb("rsum", [P, 8])
            inv = wb("inv", [P, 2, NT])
            osum = wb("osum", [P, 2, NT, AD])
            names = ("s_ps", "mx_ok", "sm_ok", "pr_ok", "t_ps", "hi_ok", "lo_ok", "o_ps", "osum_ok", "o_ok", "inv_ok", "mask_ok", "bo_ok", "gap", "gap_p")
            D = {n: sem("d_" + n) for n in names}
            UN = 8
            TURNS = AH * NB // 2
            block = work.enter_context(nc.Block())

            def wait(eng, s, base, k):
                if not isinstance(base, int) or base + k > 0:
                    eng.wait_ge(s, base + k)

            def turns(eng, turn):
                turn(0, (0, 0), None)
                with eng.Fori(1, NB // 2) as g:
                    turn(g, (0, g), (0, g - 1))
                with eng.Fori(1, AH) as h:
                    turn(h * (NB // 2), (h, 0), (h - 1, NB // 2 - 1))
                    with eng.Fori(1, NB // 2) as g:
                        turn(h * (NB // 2) + g, (h, g), (h, g - 1))
                turn(TURNS, None, (AH - 1, NB // 2 - 1))

            @block.sync
            def _(sp):
                def turn(it, here, before):
                    if here is None:
                        return
                    h, g = here
                    for j in range(2):
                        wait(sp, D["s_ps"], it * UN, -UN + 4 * j + 4)
                        if not isinstance(it, int):
                            load_qk(sp, h, g, j)
                turns(sp, turn)

            @block.tensor
            def _(pe):
                def turn(it, here, before):
                    n = it * UN
                    for u in range(UN):
                        if here is not None:
                            j, qt = u // 4, u % 4
                            if qt == 0:
                                pe.wait_ge(qk_in[j], it * 96 + 96)
                            wait(pe, D["mx_ok"], n, u - 1)
                            pe.matmul(banks[u % 2][:], qx[:, j, qt * P:(qt + 1) * P], kx[:, j], start=True,
                                      stop=True).then_inc(D["s_ps"], 1)
                        if before is not None or u >= 2:
                            if here is not None or u < 2:
                                v = (u - 2) % 4
                                pe.wait_ge(D["pr_ok"], n + u - 1)
                                wait(pe, D["lo_ok"], n, u - 5)
                                for kt in range(NT):
                                    i = pe.transpose(banks[2 + v][:, kt * P:(kt + 1) * P], pr[:, v, kt * P:(kt + 1) * P], ident[:])
                                i.then_inc(D["t_ps"], 1)
                        if (before is not None or u >= 5) and (here is not None or u < 5):
                            v = (u - 5) % 4
                            h, g = here if u >= 5 else before
                            j = 1 if 1 <= u < 5 else 0
                            pe.wait_ge(D["lo_ok"], n + u - 4)
                            pe.wait_ge(D["hi_ok"], n + u - 4)
                            if v == 0:
                                pe.wait_ge(D["osum_ok"], it * 2 + (1 if u >= 5 else 0))
                            for kt in range(NT):
                                vv = v3[:, bass.ds((g * 2 + j) * NT + kt, 1), :, bass.ds(h * AD, AD)].rearrange("p a c d -> p (a c) d")
                                for part in (hi, lo):
                                    i = pe.matmul(banks[6 + j][:, v * 3 * AD:(v + 1) * 3 * AD], part[:, v, kt * P:(kt + 1) * P], vv,
                                                  start=(kt == 0 and part is hi and v == 0), stop=True, skip_group_check=True)
                            i.then_inc(D["o_ps"], 1)
                turns(pe, turn)

            @block.scalar
            def _(act):
                nc.scalar.preload_act_table(ACT.Exp)

                def turn(it, here, before):
                    n = it * UN
                    for u in range(UN):
                        if here is not None:
                            v = u % 4
                            act.wait_ge(D["sm_ok"], n + u + 1)
                            wait(act, D["t_ps"], n, u - 3)
                            nc.scalar.activation(pr[:, v], sm[:, v], ACT.Exp, bias=nmx[:, v:v + 1],
                                                 accum_out=rsum[:, u:u + 1]).then_inc(D["pr_ok"], 1)
                        if (before is not None or u >= 2) and (here is not None or u < 2):
                            v = (u - 2) % 4
                            act.wait_ge(D["t_ps"], n + u - 1)
                            wait(act, D["o_ps"], n, u - 5)
                            nc.scalar.copy(hi[:, v], banks[2 + v][:]).then_inc(D["hi_ok"], 1)
                turns(act, turn)

            @block.vector
            def _(dve):
                def outputs(k, j):
                    dve.wait_ge(D["o_ps"], 4 * k)
                    dve.wait_ge(D["o_ok"], k)
                    o = banks[6 + j][:, 0:NT * 3 * AD].rearrange("p (t c d) -> p t d c", t=NT, c=3)
                    nc.vector.tensor_reduce(osum[:, j], o, AX, ALU.add).then_inc(D["osum_ok"], 1)

                def turn(it, here, before):
                    n = it * UN
                    if here is not None and (isinstance(here[1], int) and here[1] == 0):
                        wait(dve, D["mx_ok"], n, 0)
                        mb = m_cur[:]
                        nc.vector.tensor_copy(bass.AP(tensor=mb.tensor, offset=mb.offset + MW - 1, ap=[list(mb.ap[0]), [-1, MW]]),
                                              mask[:, bass.ds(here[0], 1)].rearrange("p a c -> p (a c)")).then_inc(D["mask_ok"], 1)
                        dve.wait_ge(D["mask_ok"], here[0] + 1)
                    for u in range(UN):
                        if here is not None:
                            v, qt = u % 4, u % 4
                            dve.wait_ge(D["s_ps"], n + u + 1)
                            wait(dve, D["pr_ok"], n, u - 3)
                            dve.sem_inc(D["gap"], 1)
                            first = (NT - 1 - qt) * P
                            nc.vector.tensor_tensor_reduce(sm[:, v], banks[u % 2][:], m_cur[:, first:first + S], 1.0, -3e38,
                                                           ALU.mult, ALU.max, mx[:, v:v + 1]).then_inc(D["mx_ok"], 1)
                        if (before is not None or u >= 4) and (here is not None or u < 4):
                            w = (u - 4) % 4
                            dve.wait_ge(D["hi_ok"], n + u - 3)
                            wait(dve, D["o_ps"], n, u - 7)
                            nc.vector.tensor_tensor(lo[:, w], banks[2 + w][:], hi[:, w], ALU.subtract).then_inc(D["lo_ok"], 1)
                        if u == 1 and before is not None:
                            outputs(it * 2 - 1, 0)
                        if u == 2 and before is not None:
                            dve.wait_ge(D["pr_ok"], n)
                            dve.wait_ge(D["o_ok"], it * 2)
                            nc.vector.reciprocal(inv[:, 1], rsum[:, 4:8]).then_inc(D["inv_ok"], 1)
                        if u == 5 and before is not None:
                            outputs(it * 2, 1)
                        if u == 6 and here is not None:
                            dve.wait_ge(D["pr_ok"], n + 4)
                            dve.wait_ge(D["o_ok"], it * 2 + 1)
                            nc.vector.reciprocal(inv[:, 0], rsum[:, 0:4]).then_inc(D["inv_ok"], 1)
                dve.sem_inc(D["osum_ok"], 2)
                turns(dve, turn)

            @block.gpsimd
            def _(pool):
                def divided(k, h, g, j):
                    pool.wait_ge(D["osum_ok"], k + 2)
                    pool.wait_ge(D["inv_ok"], k)
                    nc.gpsimd.tensor_tensor(att[:, bass.ds((g * 2 + j) * NT, NT), bass.ds(h * AD, AD)], osum[:, j],
                                            inv[:, j].unsqueeze(2).broadcast_to([P, NT, AD]), ALU.mult).then_inc(D["o_ok"], 1)

                def turn(it, here, before):
                    n = it * UN
                    for u in range(UN):
                        if here is not None:
                            v = u % 4
                            pool.wait_ge(D["mx_ok"], n + u + 1)
                            wait(pool, D["pr_ok"], n, u - 3)
                            pool.sem_inc(D["gap_p"], 1)
                            nc.gpsimd.tensor_scalar(nmx[:, v:v + 1], mx[:, v:v + 1], -1.0, None, ALU.mult).then_inc(D["sm_ok"], 1)
                        if isinstance(it, int) and it == 0:
                            xb = x1[:, u * NT:(u + 1) * NT]
                            nc.gpsimd.tensor_tensor(xb, xb, bo_row[:].unsqueeze(1).broadcast_to([P, NT, DM]),
                                                    ALU.add).then_inc(D["bo_ok"], 1)
                        if u == 2 and before is not None:
                            divided(it * 2 - 1, *before, 0)
                        if u == 6 and before is not None:
                            divided(it * 2, *before, 1)
                pool.sem_inc(D["o_ok"], 2)
                turns(pool, turn)

        with ExitStack() as work:
            wb = in_scope(work)
            aT = wb("aT", [P, 2, S])
            names = ("aT_ps", "aT_ok", "y_ps", "x_ok", "done")
            F = {n: sem("e_" + n) for n in names}
            out_v = out.rearrange("b (t p) d -> p b t d", p=P)
            block = work.enter_context(nc.Block())

            @block.tensor
            def _(pe):
                def turned(b):
                    if b >= 2:
                        pe.wait_ge(F["aT_ok"], b - 1)
                    for t in range(NT):
                        i = pe.transpose(banks[b % 2][:, t * P:(t + 1) * P], att[:, b * NT + t], ident[:])
                    i.then_inc(F["aT_ps"], 1)

                turned(0)
                for b in range(NB):
                    if b + 1 < NB:
                        turned(b + 1)
                    pe.wait_ge(F["aT_ok"], b + 1)
                    if b >= 2:
                        pe.wait_ge(F["x_ok"], b - 1)
                    for t in range(NT):
                        i = pe.matmul(banks[2 + b % 2][:, t * P:(t + 1) * P], aT[:, b % 2, t * P:(t + 1) * P], w_att[:], start=True, stop=True)
                    i.then_inc(F["y_ps"], 1)

            @block.scalar
            def _(act):
                for b in range(NB):
                    act.wait_ge(F["aT_ps"], b + 1)
                    if b >= 2:
                        act.wait_ge(F["y_ps"], b - 1)
                    nc.scalar.copy(aT[:, b % 2], banks[b % 2][:]).then_inc(F["aT_ok"], 1)

            @block.vector
            def _(dve):
                for b in range(NB):
                    dve.wait_ge(F["y_ps"], b + 1)
                    xb = x1[:, b * NT:(b + 1) * NT].rearrange("p t d -> p (t d)")
                    nc.vector.tensor_tensor(xb, banks[2 + b % 2][:], xb, ALU.add).then_inc(F["x_ok"], 1)

            @block.sync
            def _(sp):
                for b in range(NB):
                    sp.wait_ge(F["x_ok"], b + 1)
                    sp.dma_start(out_v[:, b], x1[:, b * NT:(b + 1) * NT]).then_inc(F["done"], 16)
                sp.wait_ge(F["done"], 16 * NB)


def layout(inputs):
    import numpy as np
    a = {k: np.asarray(v) for k, v in inputs.items()}
    t = lambda n: np.ascontiguousarray(a[n].T)
    lay = {"x": a["L0_attn_x"], "in_wT": t("L0_attn_in_proj_w"), "out_wT": t("L0_attn_out_proj_w"),
           "router_wT": t("L0_ffn_router_w"), "experts_bias": a["L0_ffn_experts_bias"],
           "wqT": np.ascontiguousarray(a["L1_attn_Wq"].T), "wkT": np.ascontiguousarray(a["L1_attn_Wk"].T),
           "wvT": np.ascontiguousarray(a["L1_attn_Wv"].T), "woT": np.ascontiguousarray(a["L1_attn_Wo"].T),
           "gate_wT": t("L1_ffn_gate_w"), "gate_b": a["L1_ffn_gate_b"],
           "expert_w": a["L1_ffn_expert_w"], "expert_b": a["L1_ffn_expert_b"],
           "ident": np.eye(P, dtype=np.float32)}
    for n in ("bq", "bk", "bv", "bo", "decay_params", "mix_weights"):
        lay[n] = a["L1_attn_" + n]
    for n in ("w1", "w3", "w2", "sw1", "sw3", "sw2"):
        lay[n] = a["L0_ffn_" + n]
    for n in ("A_log", "dt_bias", "Dparam", "ln_w", "ln_b", "ni_w", "ni_b", "no_w", "no_b"):
        lay[n] = a["L0_attn_" + n]
    for n in ("ln_w", "ln_b", "bq", "bk"):
        lay[n] = np.ascontiguousarray(lay[n].reshape(-1, P).T)
    return lay


def kernel(**inputs):
    import numpy as np
    import concourse.bacc as bacc
    from concourse.bass_utils import run_bass_kernel_spmd

    nc = bacc.Bacc("TRN2", target_bir_lowering=False, num_devices=1)
    arrays = layout(inputs)
    ins = {n: nc.dram_tensor(f"in_{n}", a.shape, mybir.dt.from_np(a.dtype), kind="ExternalInput").ap()
           for n, a in arrays.items()}
    out = nc.dram_tensor("out", (NB, S, DM), F32, kind="ExternalOutput").ap()
    two_layers_kernel(nc, ins, out)
    result = run_bass_kernel_spmd(nc, [{f"in_{n}": a for n, a in arrays.items()}], core_ids=[0])
    return result.results[0]["out"]
```
